# Optimizing a Trainium2 kernel written in Bass

```python
import numpy as np
import jax
import jax.numpy as jnp

def _softmax(x, axis=-1):
    return jax.nn.softmax(x, axis=axis)

def _gelu(x):
    return jax.nn.gelu(x, approximate=True)

def _silu(x):
    return jax.nn.silu(x)

def _sigmoid(x):
    return jax.nn.sigmoid(x)

def _layernorm(x, axis=-1, eps=1e-05):
    m = jnp.mean(x, axis=axis, keepdims=True)
    v = jnp.var(x, axis=axis, keepdims=True)
    return (x - m) / jnp.sqrt(v + eps)

def _scatter_add(tgt, idx, src, axis=0):
    return tgt.at[idx].add(src)

def _segment_sum(src, seg, n):
    return jax.ops.segment_sum(src, seg, n)
kernel_name = 'mk_prb_d1_jaxref_r8_68d156'

def setup_inputs(seed: int=0):
    np.random.seed(seed)
    _w = jnp.asarray

    def _L0_attn_setup():
        import jax, jax.numpy as jnp
        import numpy as np
        EPS = 1e-06

        def rms(z):
            return z / jnp.sqrt(jnp.mean(z * z, axis=-1, keepdims=True) + EPS)

        def polar_orthogonal(W, iters=12):
            X = W / (jnp.linalg.norm(W) + 1e-08)

            def body(X, _):
                Xn = 1.5 * X - 0.5 * (X @ X.T @ X)
                return (Xn, None)
            X, _ = jax.lax.scan(body, X, None, length=iters)
            return X

        def _reference_tuple_inner(x, Wq, Wv, Wc, identity, W_lh, W_rh):
            B, T, C = x.shape
            O_lh = polar_orthogonal(W_lh)
            O_rh = polar_orthogonal(W_rh)
            q = jnp.einsum('btc,dc->btd', x, Wq)
            v = jnp.einsum('btc,dc->btd', x, Wv)

            def step(h, q_t):
                h_new = rms(h @ O_lh.T + q_t @ O_rh.T)
                return (h_new, h_new)
            h0 = jnp.broadcast_to(identity, (B, C))
            _, qs = jax.lax.scan(step, h0, jnp.swapaxes(q, 0, 1))
            qs = jnp.swapaxes(qs, 0, 1)
            Y = jnp.einsum('btc,dc->btd', qs * v, Wc)
            return (Y, qs)
        key = jax.random.key(seed)
        ks = jax.random.split(key, 8)
        B, T, C = (4, 512, 128)
        s = 1.0 / np.sqrt(C)
        x = jax.random.normal(ks[0], (B, T, C), dtype=jnp.float32)
        Wq = jax.random.normal(ks[1], (C, C), dtype=jnp.float32) * s
        Wv = jax.random.normal(ks[2], (C, C), dtype=jnp.float32) * s
        Wc = jax.random.normal(ks[3], (C, C), dtype=jnp.float32) * s
        identity = jax.random.uniform(ks[4], (C,), dtype=jnp.float32)
        W_lh = jax.random.normal(ks[5], (C, C), dtype=jnp.float32) * s
        W_rh = jax.random.normal(ks[6], (C, C), dtype=jnp.float32) * s
        return {'x': x, 'Wq': Wq, 'Wv': Wv, 'Wc': Wc, 'identity': identity, 'W_lh': W_lh, 'W_rh': W_rh}
    _L0_attn_in = _L0_attn_setup()

    def _L0_ffn_setup():
        import jax, jax.numpy as jnp
        import numpy as np
        INPUT_SIZE = 128
        OUTPUT_SIZE = 128
        key = jax.random.key(seed)
        kx, kt, kp, ktn, kpn = jax.random.split(key, 5)
        x = jax.random.normal(kx, (8, 256, INPUT_SIZE), dtype=jnp.float32)
        theta = jax.random.normal(kt, (INPUT_SIZE, OUTPUT_SIZE), dtype=jnp.float32) * 0.02
        phi = jax.random.normal(kp, (INPUT_SIZE, OUTPUT_SIZE), dtype=jnp.float32) * 0.02
        theta_noise = jax.random.normal(ktn, (INPUT_SIZE, OUTPUT_SIZE), dtype=jnp.float32) * 0.01
        phi_noise = jax.random.normal(kpn, (INPUT_SIZE, OUTPUT_SIZE), dtype=jnp.float32) * 0.01
        return {'x': x, 'theta': theta, 'phi': phi, 'theta_noise': theta_noise, 'phi_noise': phi_noise}
    _L0_ffn_in = _L0_ffn_setup()
    _d = {'L0_attn_x': _L0_attn_in['x'], 'L0_attn_Wq': _L0_attn_in['Wq'], 'L0_attn_Wv': _L0_attn_in['Wv'], 'L0_attn_Wc': _L0_attn_in['Wc'], 'L0_attn_identity': _L0_attn_in['identity'], 'L0_attn_W_lh': _L0_attn_in['W_lh'], 'L0_attn_W_rh': _L0_attn_in['W_rh'], 'L0_ffn_theta': _L0_ffn_in['theta'], 'L0_ffn_phi': _L0_ffn_in['phi'], 'L0_ffn_theta_noise': _L0_ffn_in['theta_noise'], 'L0_ffn_phi_noise': _L0_ffn_in['phi_noise']}
    _x0 = _d['L0_attn_x']
    _d['L0_attn_x'] = jax.random.normal(jax.random.fold_in(jax.random.key(seed), 1), (8, 512, 128), dtype=_x0.dtype)
    del _x0
    return _d

def reference(L0_attn_x, L0_attn_Wq, L0_attn_Wv, L0_attn_Wc, L0_attn_identity, L0_attn_W_lh, L0_attn_W_rh, L0_ffn_theta, L0_ffn_phi, L0_ffn_theta_noise, L0_ffn_phi_noise):

    def _L0_attn_ref(x, Wq, Wv, Wc, identity, W_lh, W_rh):
        import jax, jax.numpy as jnp
        import numpy as np
        EPS = 1e-06

        def rms(z):
            return z / jnp.sqrt(jnp.mean(z * z, axis=-1, keepdims=True) + EPS)

        def polar_orthogonal(W, iters=12):
            X = W / (jnp.linalg.norm(W) + 1e-08)

            def body(X, _):
                Xn = 1.5 * X - 0.5 * (X @ X.T @ X)
                return (Xn, None)
            X, _ = jax.lax.scan(body, X, None, length=iters)
            return X

        def _reference_tuple_inner(x, Wq, Wv, Wc, identity, W_lh, W_rh):
            B, T, C = x.shape
            O_lh = polar_orthogonal(W_lh)
            O_rh = polar_orthogonal(W_rh)
            q = jnp.einsum('btc,dc->btd', x, Wq)
            v = jnp.einsum('btc,dc->btd', x, Wv)

            def step(h, q_t):
                h_new = rms(h @ O_lh.T + q_t @ O_rh.T)
                return (h_new, h_new)
            h0 = jnp.broadcast_to(identity, (B, C))
            _, qs = jax.lax.scan(step, h0, jnp.swapaxes(q, 0, 1))
            qs = jnp.swapaxes(qs, 0, 1)
            Y = jnp.einsum('btc,dc->btd', qs * v, Wc)
            return (Y, qs)
        return _reference_tuple_inner(x, Wq, Wv, Wc, identity, W_lh, W_rh)[0]

    def _L0_ffn_ref(x, theta, phi, theta_noise, phi_noise):
        import jax, jax.numpy as jnp
        import numpy as np
        INPUT_SIZE = 128
        OUTPUT_SIZE = 128
        real = jnp.einsum('bti,io->bto', x, jnp.cos(theta + theta_noise))
        imag = jnp.einsum('bti,io->bto', x, jnp.sin(phi + phi_noise))
        return jnp.sqrt(real * real + imag * imag)
    x = L0_attn_x
    xn = _layernorm(x, axis=-1)
    x = x + _L0_attn_ref(xn, L0_attn_Wq, L0_attn_Wv, L0_attn_Wc, L0_attn_identity, L0_attn_W_lh, L0_attn_W_rh) + _L0_ffn_ref(xn, L0_ffn_theta, L0_ffn_phi, L0_ffn_theta_noise, L0_ffn_phi_noise)
    return x

_drawn_inputs = setup_inputs


def setup_inputs(seed=0):
    import zlib

    import numpy as np

    out = dict(_drawn_inputs(seed))
    spreads = {}
    factors = {'L0_attn_identity': 4.661, 'L0_ffn_theta': 8.0, 'L0_ffn_theta_noise': 8.0}
    for name, (base, spread) in spreads.items():
        noise = np.random.default_rng([zlib.crc32(name.encode()), seed]).standard_normal(out[name].shape)
        drawn = base * np.exp(spread * noise) if base else spread * noise
        out[name] = jnp.asarray(drawn.astype(out[name].dtype))
    for name, factor in factors.items():
        out[name] = (out[name] * factor).astype(out[name].dtype)
    return out
```

```python
from contextlib import ExitStack
import math

import concourse.bass as bass
from concourse import mybir

ALU = mybir.AluOpType
ACT = mybir.ActivationFunctionType
F32 = mybir.dt.float32
I32 = mybir.dt.int32
AX = mybir.AxisListType

LN_EPS = 1e-5
RMS_EPS = 1e-6
NORM_EPS = 1e-8
POLAR_ITERS = 12

STEPS = 16
WARM = 4
TOL = 4e-6

TWO_PI_A = 6.28125
TWO_PI_B = 0.0019350051879882812
TWO_PI_C = 2.0 * math.pi - TWO_PI_A - TWO_PI_B
ROUND = 12582912.0
SIN_MAX = 3.1415925


def bass_layer(nc, x, Wq, Wv, Wc, identity, W_lh, W_rh, theta, phi, theta_noise, phi_noise, out):
    B, T, C = x.shape
    P = C
    NCHUNK = T // STEPS
    GROUPS = B * NCHUNK // P
    GB = B // GROUPS
    TILES = GROUPS * STEPS
    GW = GROUPS * P
    assert P == 128 and GROUPS == 2 and GB * NCHUNK == P
    BANK = 512

    ctx = ExitStack()
    with ctx:
        def sb(name, shape, dt=F32):
            return ctx.enter_context(nc.sbuf_tensor(name, shape, dt))

        def sem(name):
            return ctx.enter_context(nc.semaphore(name))

        bank = [ctx.enter_context(nc.psum_tensor(f"bank{i}", [P, BANK], F32)) for i in range(8)]

        X = sb("X", [P, GROUPS, STEPS, C])
        XN = sb("XN", [P, GROUPS, STEPS, C])
        XNT = sb("XNT", [P, STEPS * GW])
        UT = sb("UT", [P, STEPS * GW])
        VT = sb("VT", [P, STEPS * GW])
        WT = sb("WT", [P, STEPS * GW])
        RT = sb("RT", [P, STEPS * GW])
        OUT = sb("OUT", [P, GROUPS, STEPS, C])
        EDGE = [sb(f"EDGE{g}", [P, GB, NCHUNK + 1]) for g in range(GROUPS)]
        EDGE_RI = [sb(f"EDGE_RI{g}", [P, GB, NCHUNK + 1]) for g in range(GROUPS)]
        START = [sb(f"START{g}", [P, P]) for g in range(GROUPS)]
        SQ = [sb(f"SQ{g}", [P, P]) for g in range(GROUPS)]
        MIX = [sb(f"MIX{g}", [P, P]) for g in range(GROUPS)]
        Q = [sb(f"Q{g}", [1, P]) for g in range(GROUPS)]
        MV = sb("MV", [P, TILES, 2])
        STATS = sb("STATS", [P, TILES, 6])
        RSTD = sb("RSTD", [P, TILES])
        SD = sb("SD", [P, TILES])
        WQ = sb("WQ", [P, P])
        WV = sb("WV", [P, P])
        WC = sb("WC", [P, P])
        WVT = sb("WVT", [P, P])
        WCT = sb("WCT", [P, P])
        MT = sb("MT", [P, P])
        WP = [sb(f"WP{m}", [P, P]) for m in range(2)]
        PX = [sb(f"PX{m}", [P, P]) for m in range(2)]
        PXT = [sb(f"PXT{m}", [P, P]) for m in range(2)]
        PP = [sb(f"PP{m}", [P, P]) for m in range(2)]
        SSW = sb("SSW", [P, 2])
        NRM = sb("NRM", [P, 2])
        NRE = sb("NRE", [P, 2])
        NRI = sb("NRI", [P, 2])
        H0 = sb("H0", [P, 1])
        IDENT = sb("IDENT", [P, P])
        IDENT15 = sb("IDENT15", [P, P])
        MEAN = sb("MEAN", [P, P])
        ONES = sb("ONES", [P, P])
        ONE_ROW = sb("ONE_ROW", [1, P])
        EPS_ROW = sb("EPS_ROW", [1, P])
        EPS_LN = sb("EPS_LN", [P, 1])
        ANG = sb("ANG", [P, 2, P])
        NOISE = sb("NOISE", [P, 2, P])
        TURN = sb("TURN", [P, 2, P])
        CS = sb("CS", [P, 2 * P])
        FSQ = sb("FSQ", [P, 2, BANK])
        FS = sb("FS", [P, 2, 2, P])
        FR = sb("FR", [P, 2, 2, P])
        RINV = sb("RINV", [P, TILES])
        DIFF = [sb(f"DIFF{g}", [P, P]) for g in range(GROUPS)]
        SAME = sb("SAME", [P, GROUPS])
        SAMES = sb("SAMES", [1, GROUPS])
        FLAG = sb("FLAG", [1, 2], I32)

        x_view = x.rearrange("(g b) (k j) c -> g (b k) j c", g=GROUPS, j=STEPS)
        out_view = out.rearrange("(g b) (k j) c -> g (b k) j c", g=GROUPS, j=STEPS)
        XQ = 4
        QS = STEPS // XQ

        names = """w_loaded h0_loaded ang_loaded consts_ready ident_ready
            polar_ss polar_tot polar_nrm polar_inv polar_nre w_transposed wt_copied
            gram_done pp_done next_done px_copied pxt_copied
            stats_done mv_done sd_done rstd_done xn_done xt_done xt_copied mt_done mt_copied
            u_done u_copied v_done v_copied ang_sum turn_a turn_b turn_c turn_d turn_e cs_done
            ffn_done ffn_sq ffn_sum ffn_root xf_done
            edge_init start_saved pv_done rt_done rinv_done y_done out_done
            same_e same_d same_q same_done same_tot flag_ready stored edge_same""".split()
        S = {n: sem(n) for n in names}
        x_loaded = [sem(f"x_loaded{q}") for q in range(XQ)]
        w_ready = [sem(f"w_ready{g}") for g in range(GROUPS)]
        y_ready = [sem(f"y_ready{g}") for g in range(GROUPS)]
        m_ready = [sem(f"m_ready{g}") for g in range(GROUPS)]
        sq_ready = [sem(f"sq_ready{g}") for g in range(GROUPS)]
        q_ready = [sem(f"q_ready{g}") for g in range(GROUPS)]
        s_ready = [sem(f"s_ready{g}") for g in range(GROUPS)]
        r_ready = [sem(f"r_ready{g}") for g in range(GROUPS)]
        ri_ready = [sem(f"ri_ready{g}") for g in range(GROUPS)]

        Y = [bank[0], bank[1]]
        SUM = [bank[2], bank[3]]
        FILL = bank[4:8]
        GRAM = [bank[0], bank[1]]
        NEXT = [bank[2], bank[3]]
        NEXTT = [bank[4], bank[5]]
        PRE = [bank[6], bank[7]]

        def cols(j, g):
            return bass.ds(j * GW + g * P, P)

        def edge_new(buf):
            return buf[:, :, 1:NCHUNK + 1]

        def edge_old(buf):
            return buf[:, :, 0:NCHUNK]

        def split(ap):
            return ap.rearrange("p (b k) -> p b k", b=GB)

        def state(j, g):
            return edge_new(EDGE[g]) if j is LAST else WT[:, cols(j, g)]

        LAST = "last"

        block = ctx.enter_context(nc.Block())

        @block.sync
        def _(sp):
            for src, dst in ((W_lh, WP[0]), (W_rh, WP[1]), (Wq, WQ), (Wv, WV), (Wc, WC)):
                sp.dma_start(dst[:, :], src).then_inc(S["w_loaded"], 16)
            for q in range(XQ):
                for g in range(GROUPS):
                    sp.dma_start(X[:, g, q * QS:(q + 1) * QS, :],
                                 x_view[g, :, q * QS:(q + 1) * QS, :]).then_inc(x_loaded[q], 16)

            def store(t):
                for j in range(QS, STEPS + 1, QS):
                    sp.wait_ge(S["out_done"], t * TILES + j * GROUPS)
                    for g in range(GROUPS):
                        sp.dma_start(out_view[g, :, j - QS:j, :],
                                     OUT[:, g, j - QS:j, :]).then_inc(S["stored"], 16)
                sp.wait_ge(S["stored"], 16 * (t + 1) * XQ * GROUPS)

            store(0)
            sp.wait_ge(S["flag_ready"], 1)
            more = sp.value_load(FLAG[0:1, 0:1], min_val=0, max_val=1)
            with sp.If(more > 0):
                store(1)
            sp.end_ifs()

        @block.gpsimd
        def _(pool):
            pool.memset(IDENT[:, :], 0.0).then_inc(S["ident_ready"], 1)
            pool.wait_ge(S["ident_ready"], 1)
            pool.affine_select(out=IDENT[:, :], in_=IDENT[:, :], compare_op=ALU.not_equal, fill=1.0, base=0,
                               pattern=[[-1, P]], channel_multiplier=1).then_inc(S["ident_ready"], 1)

            def pass_pool(p):
                for g in range(GROUPS):
                    pool.wait_ge(ri_ready[g], p + 1)
                    pool.tensor_tensor(split(START[g][:, :]), edge_new(EDGE[g]), edge_new(EDGE_RI[g]),
                                       ALU.mult).then_inc(S["start_saved"], 1)
                for j in range(STEPS - 1):
                    for g in range(GROUPS):
                        pool.wait_ge(r_ready[g], p * STEPS + j + 1)
                        pool.tensor_tensor(Q[g][:, :], RT[0:1, cols(j, g)], RT[0:1, cols(j, g)],
                                           ALU.mult).then_inc(q_ready[g], 1)

            pool.wait_ge(S["edge_init"], 5)
            with pool.Fori(0, WARM) as p:
                pass_pool(p)
            pool.wait_ge(S["flag_ready"], 1)
            more = pool.value_load(FLAG[0:1, 0:1], min_val=0, max_val=1)
            with pool.If(more > 0):
                with pool.Fori(WARM, NCHUNK) as p:
                    pass_pool(p)
            pool.end_ifs()

        @block.scalar
        def _(act):
            for src, dst in ((theta, ANG[:, 0, :]), (phi, ANG[:, 1, :]),
                             (theta_noise, NOISE[:, 0, :]), (phi_noise, NOISE[:, 1, :])):
                act.dma_start(dst, src).then_inc(S["ang_loaded"], 16)
            act.dma_start(H0[:, :], identity.rearrange("(c a) -> c a", a=1)).then_inc(S["h0_loaded"], 16)
            act.wait_ge(S["turn_e"], 1)
            act.activation(CS[:, :], ANG[:, :, :].rearrange("p a n -> p (a n)"), ACT.Sin).then_inc(S["cs_done"], 1)
            act.wait_ge(S["polar_tot"], 1)
            act.activation(NRM[:, :], PRE[0][:, 0:2], ACT.Sqrt).then_inc(S["polar_nrm"], 1)

            def polar(it):
                for m in range(2):
                    act.wait_ge(S["next_done"], it * 4 + 2 * m + 2)
                    act.copy(PX[m][:, :], NEXT[m][:, 0:P]).then_inc(S["px_copied"], 1)

            with act.Fori(0, POLAR_ITERS) as it:
                polar(it)
            for q in range(XQ):
                act.wait_ge(S["mv_done"], (q + 1) * QS * GROUPS)
                sl = slice(q * QS * GROUPS, (q + 1) * QS * GROUPS)
                act.activation(SD[:, sl], MV[:, sl, 1:2].rearrange("p t o -> p (t o)"), ACT.Sqrt,
                               bias=EPS_LN[:, :]).then_inc(S["sd_done"], 1)
            for i in range(TILES // 4):
                act.wait_ge(S["xt_done"], i + 1)
                act.copy(XNT[:, i * BANK:(i + 1) * BANK], PRE[i % 2][:, :]).then_inc(S["xt_copied"], 1)
            for i in range(TILES // 4):
                act.wait_ge(S["u_done"], i + 1)
                act.copy(UT[:, i * BANK:(i + 1) * BANK], FILL[i % 2][:, :]).then_inc(S["u_copied"], 1)
                act.wait_ge(S["v_done"], i + 1)
                act.copy(VT[:, i * BANK:(i + 1) * BANK], FILL[2 + i % 2][:, :]).then_inc(S["v_copied"], 1)
            for i in range(TILES // 2):
                act.wait_ge(S["ffn_done"], i + 1)
                if i >= 2:
                    act.wait_ge(S["ffn_sum"], i - 1)
                act.activation(FSQ[:, i % 2, :], FILL[i % 2][:, :], ACT.Square).then_inc(S["ffn_sq"], 1)
                act.wait_ge(S["ffn_sum"], i + 1)
                if i >= 2:
                    act.wait_ge(S["xf_done"], i - 1)
                act.activation(FR[:, i % 2], FS[:, i % 2], ACT.Sqrt).then_inc(S["ffn_root"], 1)

            def pass_act(p):
                for j in range(STEPS):
                    n = p * STEPS + j
                    for g in range(GROUPS):
                        w = edge_new(EDGE[g]) if j == STEPS - 1 else split(WT[:, cols(j, g)])
                        act.wait_ge(w_ready[g], n + 1)
                        act.activation(split(SQ[g][:, :]), w, ACT.Square).then_inc(sq_ready[g], 1)
                        act.wait_ge(s_ready[g], n + 1)
                        act.activation(RT[:, cols(j, g)], SUM[g][:, 0:P], ACT.Sqrt).then_inc(r_ready[g], 1)

            with act.Fori(0, WARM) as p:
                pass_act(p)
            act.wait_ge(S["flag_ready"], 1)
            more = act.value_load(FLAG[0:1, 0:1], min_val=0, max_val=1)
            with act.If(more > 0):
                with act.Fori(WARM, NCHUNK) as p:
                    pass_act(p)
            act.end_ifs()

        @block.vector
        def _(dve):
            dve.memset(ONES[:, :], 1.0).then_inc(S["consts_ready"], 1)
            dve.memset(MEAN[:, :], 1.0 / C).then_inc(S["consts_ready"], 1)
            dve.memset(ONE_ROW[:, :], 1.0).then_inc(S["consts_ready"], 1)
            dve.memset(EPS_ROW[:, :], RMS_EPS).then_inc(S["consts_ready"], 1)
            dve.memset(EPS_LN[:, :], LN_EPS).then_inc(S["consts_ready"], 1)
            for g in range(GROUPS):
                dve.memset(EDGE[g][:, :, :], 0.0).then_inc(S["edge_init"], 1)
                dve.memset(EDGE_RI[g][:, :, :], 1.0).then_inc(S["edge_init"], 1)
            dve.wait_ge(S["w_loaded"], 5 * 16)
            for m in range(2):
                dve.tensor_tensor_reduce(out=PP[m][:, :], in0=WP[m][:, :], in1=WP[m][:, :], scale=1.0, scalar=0.0,
                                         op0=ALU.mult, op1=ALU.add,
                                         accum_out=SSW[:, m:m + 1]).then_inc(S["polar_ss"], 1)
            dve.wait_ge(S["ident_ready"], 2)
            dve.tensor_scalar(IDENT15[:, :], IDENT[:, :], 1.5, None, ALU.mult).then_inc(S["consts_ready"], 1)
            dve.wait_ge(S["h0_loaded"], 16)
            dve.wait_ge(S["edge_init"], 4)
            for g in range(GROUPS):
                dve.tensor_scalar(EDGE[g][:, :, 0:1], EDGE[g][:, :, 0:1], H0[:, 0:1], None,
                                  ALU.add).then_inc(S["edge_same"], 1)
            dve.wait_ge(S["edge_same"], GROUPS)
            dve.sem_inc(S["edge_init"], 1)
            for g in range(GROUPS):
                dve.sem_inc(ri_ready[g], 1)
            dve.wait_ge(S["ang_loaded"], 4 * 16)
            dve.tensor_tensor(ANG[:, :, :], ANG[:, :, :], NOISE[:, :, :], ALU.add).then_inc(S["ang_sum"], 1)
            dve.wait_ge(S["ang_sum"], 1)
            dve.tensor_scalar(ANG[:, 0, :], ANG[:, 0, :], math.pi / 2, None, ALU.add).then_inc(S["ang_sum"], 1)
            dve.wait_ge(S["ang_sum"], 2)
            dve.tensor_scalar(TURN[:, :, :], ANG[:, :, :], 0.5 / math.pi, ROUND, ALU.mult,
                              ALU.add).then_inc(S["turn_a"], 1)
            dve.wait_ge(S["turn_a"], 1)
            dve.tensor_scalar(TURN[:, :, :], TURN[:, :, :], ROUND, None, ALU.subtract).then_inc(S["turn_b"], 1)
            dve.wait_ge(S["turn_b"], 1)
            for n, part in enumerate((TWO_PI_A, TWO_PI_B, TWO_PI_C)):
                dve.scalar_tensor_tensor(out=ANG[:, :, :], in0=TURN[:, :, :], scalar=-part, in1=ANG[:, :, :],
                                         op0=ALU.mult, op1=ALU.add).then_inc(S["turn_c"], 1)
                dve.wait_ge(S["turn_c"], n + 1)
            dve.tensor_scalar(ANG[:, :, :], ANG[:, :, :], SIN_MAX, -SIN_MAX, ALU.min,
                              ALU.max).then_inc(S["turn_e"], 1)
            dve.wait_ge(S["polar_nrm"], 1)
            dve.tensor_scalar(NRE[:, :], NRM[:, :], NORM_EPS, None, ALU.add).then_inc(S["polar_nre"], 1)
            dve.wait_ge(S["polar_nre"], 1)
            dve.reciprocal(NRI[:, :], NRE[:, :]).then_inc(S["polar_inv"], 1)
            dve.wait_ge(S["polar_inv"], 1)
            dve.wait_ge(S["w_transposed"], 1)
            for m in range(2):
                dve.tensor_scalar(PX[m][:, :], WP[m][:, :], NRI[:, m:m + 1], None,
                                  ALU.mult).then_inc(S["px_copied"], 1)
                dve.tensor_scalar(PXT[m][:, :], PRE[1][:, m * P:(m + 1) * P], NRI[:, m:m + 1], None,
                                  ALU.mult).then_inc(S["pxt_copied"], 1)
            dve.tensor_copy(WVT[:, :], PRE[1][:, 2 * P:3 * P]).then_inc(S["wt_copied"], 1)
            dve.tensor_copy(WCT[:, :], PRE[1][:, 3 * P:4 * P]).then_inc(S["wt_copied"], 1)
            with dve.Fori(0, POLAR_ITERS) as it:
                for m in range(2):
                    dve.wait_ge(S["gram_done"], it * 2 + m + 1)
                    dve.scalar_tensor_tensor(out=PP[m][:, :], in0=GRAM[m][:, 0:P], scalar=-0.5,
                                             in1=IDENT15[:, :], op0=ALU.mult, op1=ALU.add).then_inc(S["pp_done"], 1)
                for m in range(2):
                    dve.wait_ge(S["next_done"], it * 4 + 2 * m + 2)
                    dve.tensor_copy(PXT[m][:, :], NEXTT[m][:, 0:P]).then_inc(S["pxt_copied"], 1)
            for q in range(XQ):
                dve.wait_ge(x_loaded[q], 16 * GROUPS)
                tiles = [(j, g) for j in range(q * QS, (q + 1) * QS) for g in range(GROUPS)]
                for j, g in tiles:
                    t = j * GROUPS + g
                    dve.bn_stats(STATS[:, t, :], X[:, g, j, :]).then_inc(S["stats_done"], 1)
                for j, g in tiles:
                    t = j * GROUPS + g
                    dve.wait_ge(S["stats_done"], t + 1)
                    dve.bn_aggr(MV[:, t, :], STATS[:, t, :]).then_inc(S["mv_done"], 1)
                n = len(tiles)
                dve.wait_ge(S["sd_done"], q + 1)
                dve.reciprocal(RSTD[:, q * n:(q + 1) * n], SD[:, q * n:(q + 1) * n]).then_inc(S["rstd_done"], 1)
                dve.wait_ge(S["rstd_done"], q + 1)
                for j, g in tiles:
                    t = j * GROUPS + g
                    dve.tensor_scalar(XN[:, g, j, :], X[:, g, j, :], MV[:, t, 0:1], RSTD[:, t:t + 1],
                                      ALU.subtract, ALU.mult).then_inc(S["xn_done"], 1)
            dve.wait_ge(S["mt_done"], 1)
            dve.tensor_copy(MT[:, :], GRAM[0][:, 0:P]).then_inc(S["mt_copied"], 1)
            for i in range(TILES // 2):
                dve.wait_ge(S["ffn_sq"], i + 1)
                if i >= 2:
                    dve.wait_ge(S["ffn_root"], i - 1)
                sq = FSQ[:, i % 2, :].rearrange("p (t a c) -> p t a c", t=2, a=2)
                dve.tensor_tensor(FS[:, i % 2], sq[:, :, 0, :], sq[:, :, 1, :], ALU.add).then_inc(S["ffn_sum"], 1)
                dve.wait_ge(S["ffn_root"], i + 1)
                dve.tensor_tensor(XN[:, :, i, :], X[:, :, i, :], FR[:, i % 2], ALU.add).then_inc(S["xf_done"], 1)

            def pass_dve(p):
                for j in range(STEPS):
                    n = p * STEPS + j
                    for g in range(GROUPS):
                        if j == 0:
                            dve.wait_ge(ri_ready[g], p + 1)
                            dve.wait_ge(y_ready[g], n + 1)
                            dve.tensor_tensor(split(MIX[g][:, :]), split(Y[g][:, 0:P]), edge_old(EDGE_RI[g]),
                                              ALU.mult).then_inc(m_ready[g], 1)
                            dve.wait_ge(m_ready[g], n + 1)
                            dve.tensor_tensor(WT[:, cols(j, g)], MIX[g][:, :], UT[:, cols(j, g)],
                                              ALU.add).then_inc(w_ready[g], 1)
                            continue
                        dve.wait_ge(r_ready[g], n)
                        dve.tensor_tensor(MIX[g][:, :], UT[:, cols(j, g)], RT[:, cols(j - 1, g)],
                                          ALU.mult).then_inc(m_ready[g], 1)
                        dve.wait_ge(y_ready[g], n + 1)
                        dve.wait_ge(m_ready[g], n + 1)
                        if j == STEPS - 1:
                            dve.wait_ge(S["start_saved"], (p + 1) * GROUPS)
                            dve.tensor_tensor(edge_new(EDGE[g]), split(MIX[g][:, :]), split(Y[g][:, 0:P]),
                                              ALU.add).then_inc(w_ready[g], 1)
                        else:
                            dve.tensor_tensor(WT[:, cols(j, g)], MIX[g][:, :], Y[g][:, 0:P],
                                              ALU.add).then_inc(w_ready[g], 1)
                for g in range(GROUPS):
                    dve.wait_ge(r_ready[g], p * STEPS + STEPS)
                    dve.reciprocal(edge_new(EDGE_RI[g]), split(RT[:, cols(STEPS - 1, g)])).then_inc(ri_ready[g], 1)

            def tail_dve(t):
                dst = PV
                for j in range(STEPS - 1):
                    dve.tensor_tensor(dst[:, j * GW:(j + 1) * GW], VT[:, j * GW:(j + 1) * GW],
                                      WT[:, j * GW:(j + 1) * GW], ALU.mult).then_inc(S["pv_done"], 1)
                for g in range(GROUPS):
                    dve.tensor_tensor(split(dst[:, cols(STEPS - 1, g)]), split(VT[:, cols(STEPS - 1, g)]),
                                      edge_new(EDGE[g]), ALU.mult).then_inc(S["pv_done"], 1)
                dve.wait_ge(S["rt_done"], t + 1)
                dve.reciprocal(RINV[:, :], SUM[0][:, 0:TILES]).then_inc(S["rinv_done"], 1)
                dve.wait_ge(S["rinv_done"], t + 1)
                if t:
                    dve.wait_ge(S["stored"], 16 * XQ * GROUPS)
                for i in range(TILES):
                    j, g = divmod(i, GROUPS)
                    dve.wait_ge(S["y_done"], t * TILES + i + 1)
                    dve.scalar_tensor_tensor(out=OUT[:, g, j, :], in0=FILL[i % 4][:, 0:P], scalar=RINV[:, i:i + 1],
                                             in1=XN[:, g, j, :], op0=ALU.mult,
                                             op1=ALU.add).then_inc(S["out_done"], 1)

            PV = XNT
            dve.wait_ge(S["u_copied"], TILES // 4)
            dve.wait_ge(S["v_copied"], TILES // 4)
            with dve.Fori(0, WARM) as p:
                pass_dve(p)
            for g in range(GROUPS):
                dve.wait_ge(ri_ready[g], WARM + 1)
                dve.tensor_tensor(split(DIFF[g][:, :]), edge_new(EDGE[g]), edge_new(EDGE_RI[g]),
                                  ALU.mult).then_inc(S["same_e"], 1)
            for g in range(GROUPS):
                dve.wait_ge(S["same_e"], g + 1)
                dve.tensor_tensor(DIFF[g][:, :], DIFF[g][:, :], START[g][:, :], ALU.subtract).then_inc(S["same_d"], 1)
            for g in range(GROUPS):
                dve.wait_ge(S["same_d"], g + 1)
                dve.tensor_tensor(DIFF[g][:, :], DIFF[g][:, :], DIFF[g][:, :], ALU.mult).then_inc(S["same_q"], 1)
            for g in range(GROUPS):
                dve.wait_ge(S["same_q"], g + 1)
                dve.tensor_scalar(DIFF[g][:, :], DIFF[g][:, :], TOL * TOL, None, ALU.is_le, ALU.add,
                                  accum_out=SAME[:, g:g + 1]).then_inc(S["same_done"], 1)
            dve.wait_ge(S["same_tot"], 1)
            dve.tensor_copy(SAMES[:, :], SUM[1][0:1, 0:GROUPS]).then_inc(S["same_e"], 1)
            dve.wait_ge(S["same_e"], GROUPS + 1)
            dve.tensor_tensor(SAMES[:, 0:1], SAMES[:, 0:1], SAMES[:, 1:2], ALU.add).then_inc(S["same_e"], 1)
            dve.wait_ge(S["same_e"], GROUPS + 2)
            dve.tensor_scalar(FLAG[:, 0:1], SAMES[:, 0:1], GROUPS * P * P - 0.5, None,
                              ALU.is_lt).then_inc(S["flag_ready"], 1)
            tail_dve(0)
            dve.wait_ge(S["flag_ready"], 1)
            more = dve.value_load(FLAG[0:1, 0:1], min_val=0, max_val=1)
            with dve.If(more > 0):
                with dve.Fori(WARM, NCHUNK) as p:
                    pass_dve(p)
                tail_dve(1)
            dve.end_ifs()

        @block.tensor
        def _(pe):
            pe.wait_ge(S["consts_ready"], 6)
            pe.wait_ge(S["ident_ready"], 2)
            pe.wait_ge(S["w_loaded"], 5 * 16)
            pe.wait_ge(S["polar_ss"], 2)
            pe.matmul(PRE[0][:, 0:2], ONES[:, :], SSW[:, :], start=True, stop=True).then_inc(S["polar_tot"], 1)
            for i, w in enumerate((WP[0], WP[1], WV, WC)):
                last = pe.transpose(PRE[1][:, i * P:(i + 1) * P], w[:, :], IDENT[:, :])
            last.then_inc(S["w_transposed"], 1)
            with pe.Fori(0, POLAR_ITERS) as it:
                for m in range(2):
                    pe.wait_ge(S["px_copied"], it * 2 + 2)
                    pe.wait_ge(S["pxt_copied"], it * 2 + 2)
                    pe.matmul(GRAM[m][:, 0:P], PX[m][:, :], PX[m][:, :], start=True,
                              stop=True).then_inc(S["gram_done"], 1)
                for m in range(2):
                    pe.wait_ge(S["pp_done"], it * 2 + m + 1)
                    pe.matmul(NEXTT[m][:, 0:P], PP[m][:, :], PXT[m][:, :], start=True,
                              stop=True).then_inc(S["next_done"], 1)
                    pe.matmul(NEXT[m][:, 0:P], PXT[m][:, :], PP[m][:, :], start=True,
                              stop=True).then_inc(S["next_done"], 1)
            pe.wait_ge(S["wt_copied"], 2)
            for i in range(TILES // 4):
                pe.wait_ge(S["xn_done"], 4 * i + 4)
                if i >= 2:
                    pe.wait_ge(S["xt_copied"], i - 1)
                for k in range(4):
                    j, g = divmod(4 * i + k, GROUPS)
                    last = pe.transpose(PRE[i % 2][:, k * P:(k + 1) * P], XN[:, g, j, :], IDENT[:, :])
                last.then_inc(S["xt_done"], 1)
            pe.wait_ge(S["pxt_copied"], POLAR_ITERS * 2 + 2)
            pe.wait_ge(S["px_copied"], POLAR_ITERS * 2 + 2)
            pe.matmul(GRAM[0][:, 0:P], WQ[:, :], PXT[1][:, :], start=True, stop=True).then_inc(S["mt_done"], 1)
            pe.wait_ge(S["mt_copied"], 1)
            pe.wait_ge(S["xt_copied"], TILES // 4)
            for i in range(TILES // 4):
                pe.wait_ge(S["xt_copied"], i + 1)
                if i >= 2:
                    pe.wait_ge(S["u_copied"], i - 1)
                pe.matmul(FILL[i % 2][:, :], MT[:, :], XNT[:, i * BANK:(i + 1) * BANK], start=True,
                          stop=True).then_inc(S["u_done"], 1)
                if i >= 2:
                    pe.wait_ge(S["v_copied"], i - 1)
                pe.matmul(FILL[2 + i % 2][:, :], WVT[:, :], XNT[:, i * BANK:(i + 1) * BANK], start=True,
                          stop=True).then_inc(S["v_done"], 1)
            pe.wait_ge(S["cs_done"], 1)
            pe.wait_ge(S["u_copied"], TILES // 4)
            for i in range(TILES // 2):
                if i >= 2:
                    pe.wait_ge(S["ffn_sq"], i - 1)
                for g in range(GROUPS):
                    last = pe.matmul(FILL[i % 2][:, g * 2 * P:(g + 1) * 2 * P], XNT[:, cols(i, g)], CS[:, :],
                                     start=True, stop=True)
                last.then_inc(S["ffn_done"], 1)

            for g in range(GROUPS):
                pe.wait_ge(S["edge_init"], 5)
                pe.matmul(split(Y[g][:, 0:P]), PXT[0][:, :], edge_old(EDGE[g]), start=True,
                          stop=True).then_inc(y_ready[g], 1)

            def pass_pe(p):
                for j in range(STEPS):
                    n = p * STEPS + j
                    for g in range(GROUPS):
                        pe.wait_ge(w_ready[g], n + 1)
                        w = edge_old(EDGE[g]) if j == STEPS - 1 else split(WT[:, cols(j, g)])
                        pe.matmul(split(Y[g][:, 0:P]), PXT[0][:, :], w, start=True,
                                  stop=True).then_inc(y_ready[g], 1)
                        if j:
                            pe.wait_ge(q_ready[g], p * (STEPS - 1) + j)
                        q = Q[g] if j else ONE_ROW
                        pe.matmul(SUM[g][:, 0:P], EPS_ROW[:, :], q[:, :], start=True, stop=False)
                        pe.wait_ge(sq_ready[g], n + 1)
                        pe.matmul(SUM[g][:, 0:P], MEAN[:, :], SQ[g][:, :], start=False,
                                  stop=True).then_inc(s_ready[g], 1)

            def tail_pe(t):
                PV = XNT
                for g in range(GROUPS):
                    pe.wait_ge(r_ready[g], (NCHUNK if t else WARM) * STEPS)
                for i in range(TILES):
                    j, g = divmod(i, GROUPS)
                    last = pe.matmul(SUM[0][:, i:i + 1], RT[0:1, cols(j, g)], ONE_ROW[0:1, 0:1],
                                     start=True, stop=True)
                last.then_inc(S["rt_done"], 1)
                for i in range(TILES):
                    j, g = divmod(i, GROUPS)
                    if j < STEPS - 1:
                        pe.wait_ge(S["pv_done"], t * (STEPS + 1) + j + 1)
                    else:
                        pe.wait_ge(S["pv_done"], t * (STEPS + 1) + j + g + 1)
                    if t * TILES + i >= 4:
                        pe.wait_ge(S["out_done"], t * TILES + i - 3)
                    pe.matmul(FILL[i % 4][:, 0:P], PV[:, cols(j, g)], WCT[:, :], start=True,
                              stop=True).then_inc(S["y_done"], 1)

            with pe.Fori(0, WARM) as p:
                pass_pe(p)
            pe.wait_ge(S["same_done"], GROUPS)
            pe.matmul(SUM[1][:, 0:GROUPS], ONES[:, :], SAME[:, :], start=True, stop=True).then_inc(S["same_tot"], 1)
            tail_pe(0)
            pe.wait_ge(S["flag_ready"], 1)
            more = pe.value_load(FLAG[0:1, 0:1], min_val=0, max_val=1)
            with pe.If(more > 0):
                with pe.Fori(WARM, NCHUNK) as p:
                    pass_pe(p)
                tail_pe(1)
            pe.end_ifs()


_INS = ['L0_attn_x', 'L0_attn_Wq', 'L0_attn_Wv', 'L0_attn_Wc', 'L0_attn_identity', 'L0_attn_W_lh', 'L0_attn_W_rh',
        'L0_ffn_theta', 'L0_ffn_phi', 'L0_ffn_theta_noise', 'L0_ffn_phi_noise']
_OUTS = [((8, 512, 128), 'float32')]


def kernel(**inputs):
    import numpy as _np
    import concourse.bacc as _bacc
    from concourse import mybir as _mybir
    from concourse.bass_utils import run_bass_kernel_spmd as _run

    nc = _bacc.Bacc("TRN2", target_bir_lowering=False, num_devices=1)
    arrays, args = {}, []
    for name in _INS:
        a = _np.ascontiguousarray(inputs[name])
        arrays[f"in_{name}_dram"] = a
        args.append(nc.dram_tensor(f"in_{name}_dram", a.shape, _mybir.dt.from_np(a.dtype), kind="ExternalInput").ap())
    for i, (shape, dtype) in enumerate(_OUTS):
        dt = _mybir.dt.from_np(_np.dtype(dtype))
        args.append(nc.dram_tensor(f"out_{i}_dram", shape, dt, kind="ExternalOutput").ap())
    bass_layer(nc, *args)
    r = _run(nc, [arrays], core_ids=[0])
    return r.results[0]["out_0_dram"]
```

```python
from contextlib import ExitStack
import math

import concourse.bass as bass
from concourse import mybir

ALU = mybir.AluOpType
ACT = mybir.ActivationFunctionType
F32 = mybir.dt.float32
I32 = mybir.dt.int32
AX = mybir.AxisListType

LN_EPS = 1e-5
RMS_EPS = 1e-6
NORM_EPS = 1e-8
POLAR_ITERS = 12

STEPS = 16
WARM = 4
TOL = 4e-6

TWO_PI_A = 6.28125
TWO_PI_B = 0.0019350051879882812
TWO_PI_C = 2.0 * math.pi - TWO_PI_A - TWO_PI_B
ROUND = 12582912.0
SIN_MAX = 3.1415925
SIN_ITERS = 2
LN_ITER = 1


def bass_layer(nc, x, Wq, Wv, Wc, identity, W_lh, W_rh, theta, phi, theta_noise, phi_noise, out):
    B, T, C = x.shape
    P = C
    NCHUNK = T // STEPS
    GROUPS = B * NCHUNK // P
    GB = B // GROUPS
    TILES = GROUPS * STEPS
    GW = GROUPS * P
    BANK = 512
    BT = BANK // P
    BATCHES = TILES // BT
    XQ = 4
    QS = STEPS // XQ
    FFN_PASSES = 2
    FC = P // FFN_PASSES
    assert P == 128 and GROUPS == 2 and GB * NCHUNK == P and WARM == FFN_PASSES + 2

    ctx = ExitStack()
    with ctx:
        def sb(name, shape, dt=F32):
            return ctx.enter_context(nc.sbuf_tensor(name, shape, dt))

        def sem(name):
            return ctx.enter_context(nc.semaphore(name))

        bank = [ctx.enter_context(nc.psum_tensor(f"bank{i}", [P, BANK], F32)) for i in range(8)]

        X = sb("X", [P, GROUPS, STEPS, C])
        XN = sb("XN", [P, GROUPS, STEPS, C])
        XF = sb("XF", [P, GROUPS, STEPS, C])
        OUT = sb("OUT", [P, GROUPS, STEPS, C])
        XNT = sb("XNT", [P, STEPS * GW])
        UT = sb("UT", [P, STEPS * GW])
        VT = sb("VT", [P, STEPS * GW])
        WT = sb("WT", [P, STEPS * GW])
        RT = sb("RT", [P, STEPS * GW])
        EDGE = [sb(f"EDGE{g}", [P, GB, NCHUNK + 1]) for g in range(GROUPS)]
        EDGE_RI = [sb(f"EDGE_RI{g}", [P, GB, NCHUNK + 1]) for g in range(GROUPS)]
        START = [sb(f"START{g}", [P, P]) for g in range(GROUPS)]
        SQ = [sb(f"SQ{g}", [P, P]) for g in range(GROUPS)]
        MIX = [sb(f"MIX{g}", [P, P]) for g in range(GROUPS)]
        Q = [sb(f"Q{g}", [P, P]) for g in range(GROUPS)]
        DIFF = [sb(f"DIFF{g}", [P, P]) for g in range(GROUPS)]
        STATS = sb("STATS", [P, TILES, 6])
        MV = sb("MV", [P, TILES, 2])
        SD = sb("SD", [P, TILES])
        RSTD = sb("RSTD", [P, TILES])
        WQ = sb("WQ", [P, P])
        WV = sb("WV", [P, P])
        WC = sb("WC", [P, P])
        WVT = sb("WVT", [P, P])
        WCT = sb("WCT", [P, P])
        MT = sb("MT", [P, P])
        WP = [sb(f"WP{m}", [P, P]) for m in range(2)]
        PX = [sb(f"PX{m}", [P, P]) for m in range(2)]
        PXT = [[sb(f"PXT{m}_{par}", [P, P]) for m in range(2)] for par in range(2)]
        PP = [sb(f"PP{m}", [P, P]) for m in range(2)]
        SSW = sb("SSW", [P, 2])
        NRM = sb("NRM", [P, 2])
        NRE = sb("NRE", [P, 2])
        NRI = sb("NRI", [P, 2])
        H0 = sb("H0", [P, 1])
        IDENT = sb("IDENT", [P, P])
        IDENT15 = sb("IDENT15", [P, P])
        ONES_WIDE = sb("ONES_WIDE", [P, BANK])
        ONES = ONES_WIDE[:, 0:P]
        MEAN = sb("MEAN", [P, P])
        EPS_MEAN = sb("EPS_MEAN", [P, P])
        EPS_LN = sb("EPS_LN", [P, 1])
        ANG = sb("ANG", [P, 2, P])
        NOISE = sb("NOISE", [P, 2, P])
        TURN = sb("TURN", [P, 2, P])
        CS = sb("CS", [P, FFN_PASSES, 2, FC])
        FSQ = sb("FSQ", [P, 2, 2 * FC])
        FS = sb("FS", [P, 2, FC])
        FR = sb("FR", [P, 2, FC])
        PV = sb("PV", [P, 2, P])
        RINV = sb("RINV", [P, TILES])
        SAME = sb("SAME", [P, GROUPS])
        SAMES = sb("SAMES", [1, GROUPS])
        FLAG = sb("FLAG", [1, 2], I32)

        x_view = x.rearrange("(g b) (k j) c -> g (b k) j c", g=GROUPS, j=STEPS)
        out_view = out.rearrange("(g b) (k j) c -> g (b k) j c", g=GROUPS, j=STEPS)

        names = """wp_loaded w_loaded h0_loaded ang_loaded ones_ready consts_ready ident_ready id15_ready
            polar_ss polar_tot polar_nrm polar_inv polar_nre wp_transposed w_transposed wt_copied
            gram_done pp_done next_done px_copied pxt_copied
            stats_done mv_done sd_done rstd_done xn_done xt_done xt_copied mt_done mt_copied
            u_done u_copied_act u_copied_dve v_done v_copied ang_sum turn_a turn_b turn_c turn_d cs_done
            ffn_done ffn_sq ffn_sum ffn_root xf_done h0_placed edge_init start_saved
            pv_done rt_done rinv_done y_done out_done
            same_e same_d same_q same_done same_tot same_row flag_ready stored""".split()
        S = {n: sem(n) for n in names}
        x_loaded = [sem(f"x_loaded{q}") for q in range(XQ)]
        w_ready = [sem(f"w_ready{g}") for g in range(GROUPS)]
        y_ready = [sem(f"y_ready{g}") for g in range(GROUPS)]
        m_ready = [sem(f"m_ready{g}") for g in range(GROUPS)]
        sq_ready = [sem(f"sq_ready{g}") for g in range(GROUPS)]
        q_ready = [sem(f"q_ready{g}") for g in range(GROUPS)]
        s_ready = [sem(f"s_ready{g}") for g in range(GROUPS)]
        r_ready = [sem(f"r_ready{g}") for g in range(GROUPS)]
        ri_ready = [sem(f"ri_ready{g}") for g in range(GROUPS)]

        OT = PXT[POLAR_ITERS % 2]
        GRAM, NEXT, NEXTT, PRE = bank[0:2], bank[2:4], bank[4:6], bank[6:8]
        Y, SUM, SIDE, ROW_R = bank[0:2], bank[2:4], bank[4:6], bank[6:8]

        def cols(j, g):
            return slice(j * GW + g * P, j * GW + (g + 1) * P)

        def split(ap):
            return ap.rearrange("p (b k) -> p b k", b=GB)

        def edge_new(buf):
            return buf[:, :, 1:NCHUNK + 1]

        def edge_old(buf):
            return buf[:, :, 0:NCHUNK]

        def state(j, g):
            return edge_new(EDGE[g]) if j == STEPS - 1 else split(WT[:, cols(j, g)])

        LAGS = 4
        TWO = 2

        def slots():
            for n in range(TILES + LAGS):
                yield n, *divmod(n, GROUPS)

        def passes(eng, one_pass):
            with eng.Fori(0, FFN_PASSES) as p:
                one_pass(p, "ffn", 0)
            one_pass(FFN_PASSES, "v", 0)
            one_pass(WARM - 1, "out", 0)

        def more_passes(eng, one_pass):
            eng.wait_ge(S["flag_ready"], 1)
            more = eng.value_load(FLAG[0:1, 0:1], min_val=0, max_val=1)
            with eng.If(more > 0):
                with eng.Fori(WARM, NCHUNK - 1) as p:
                    one_pass(p, "", 0)
                one_pass(NCHUNK - 1, "out", 1)
            eng.end_ifs()

        block = ctx.enter_context(nc.Block())

        @block.sync
        def _(sp):
            sp.dma_start(WP[0][:, :], W_lh).then_inc(S["wp_loaded"], 16)
            for q in range(XQ):
                for g in range(GROUPS):
                    sp.dma_start(X[:, g, q * QS:(q + 1) * QS, :],
                                 x_view[g, :, q * QS:(q + 1) * QS, :]).then_inc(x_loaded[q], 16)
                if q == 0:
                    for src, dst in ((Wv, WV), (Wc, WC), (Wq, WQ)):
                        sp.dma_start(dst[:, :], src).then_inc(S["w_loaded"], 16)

            def store(t):
                for j in range(QS, STEPS + 1, QS):
                    sp.wait_ge(S["out_done"], t * TILES + j * GROUPS)
                    for g in range(GROUPS):
                        sp.dma_start(out_view[g, :, j - QS:j, :],
                                     OUT[:, g, j - QS:j, :]).then_inc(S["stored"], 16)
                sp.wait_ge(S["stored"], 16 * (t + 1) * XQ * GROUPS)

            store(0)
            sp.wait_ge(S["flag_ready"], 1)
            more = sp.value_load(FLAG[0:1, 0:1], min_val=0, max_val=1)
            with sp.If(more > 0):
                store(1)
            sp.end_ifs()

        @block.gpsimd
        def _(pool):
            pool.sem_inc(S["xf_done"], TWO)
            pool.memset(IDENT[:, :], 0.0).then_inc(S["ident_ready"], 1)
            pool.wait_ge(S["ident_ready"], 1)
            pool.affine_select(out=IDENT[:, :], in_=IDENT[:, :], compare_op=ALU.not_equal, fill=1.0, base=0,
                               pattern=[[-1, P]], channel_multiplier=1).then_inc(S["ident_ready"], 1)
            for b in range(BATCHES):
                pool.wait_ge(S["rstd_done"], b + 1)
                for t in range(b * BT, (b + 1) * BT):
                    j, g = divmod(t, GROUPS)
                    pool.tensor_scalar(XN[:, g, j, :], X[:, g, j, :], MV[:, t, 0:1], RSTD[:, t:t + 1],
                                       ALU.subtract, ALU.mult).then_inc(S["xn_done"], 1)

            def one_pass(p, side, again):
                for g in range(GROUPS):
                    pool.wait_ge(ri_ready[g], p + 1)
                    pool.tensor_tensor(split(START[g][:, :]), edge_new(EDGE[g]), edge_new(EDGE_RI[g]),
                                       ALU.mult).then_inc(S["start_saved"], 1)
                for n, j, g in slots():
                    if side == "out" and n < TILES:
                        pool.wait_ge(w_ready[g], p * STEPS + j + 1)
                        if again * TILES + n >= 2:
                            pool.wait_ge(S["y_done"], again * TILES + n - 1)
                        pool.tensor_tensor(split(PV[:, n % 2, :]), split(VT[:, cols(j, g)]), state(j, g),
                                           ALU.mult).then_inc(S["pv_done"], 1)
                    if j < STEPS - 1:
                        pool.wait_ge(r_ready[g], p * STEPS + j + 1)
                        pool.tensor_tensor(Q[g][:, :], RT[:, cols(j, g)], RT[:, cols(j, g)],
                                           ALU.mult).then_inc(q_ready[g], 1)
                    m = n - 3
                    if side == "ffn" and 0 <= m < TILES:
                        pool.wait_ge(S["ffn_root"], p * TILES + m + 1 + TWO)
                        mj, mg = divmod(m, GROUPS)
                        pool.tensor_tensor(XF[:, mg, mj, bass.ds(p * FC, FC)], X[:, mg, mj, bass.ds(p * FC, FC)],
                                           FR[:, m % 2, :], ALU.add).then_inc(S["xf_done"], 1)

            pool.wait_ge(S["edge_init"], 2 * GROUPS)
            passes(pool, one_pass)
            more_passes(pool, one_pass)

        @block.scalar
        def _(act):
            act.dma_start(WP[1][:, :], W_rh).then_inc(S["wp_loaded"], 16)
            act.sem_inc(S["ffn_sq"], TWO)
            act.sem_inc(S["ffn_root"], TWO)
            for src, dst in ((theta, ANG[:, 0, :]), (phi, ANG[:, 1, :]),
                             (theta_noise, NOISE[:, 0, :]), (phi_noise, NOISE[:, 1, :])):
                act.dma_start(dst, src).then_inc(S["ang_loaded"], 16)
            act.dma_start(H0[:, :], identity.rearrange("(c a) -> c a", a=1)).then_inc(S["h0_loaded"], 16)
            act.wait_ge(S["polar_tot"], 1)
            act.activation(NRM[:, :], PRE[0][:, 0:2], ACT.Sqrt).then_inc(S["polar_nrm"], 1)
            act.wait_ge(S["turn_d"], 1)
            for a in range(2):
                act.activation(CS[:, :, a, :], ANG[:, a, :].rearrange("p (h c) -> p h c", h=FFN_PASSES),
                               ACT.Sin).then_inc(S["cs_done"], 1)
            for it in range(SIN_ITERS, POLAR_ITERS + 2):
                b = it - LN_ITER - 1
                if 0 <= b < BATCHES:
                    act.wait_ge(S["mv_done"], (b + 1) * BT)
                    act.activation(SD[:, b * BT:(b + 1) * BT], MV[:, b * BT:(b + 1) * BT, 1:2], ACT.Sqrt,
                                   bias=EPS_LN[:, :]).then_inc(S["sd_done"], 1)
                if it < POLAR_ITERS - 1:
                    for m in range(2):
                        act.wait_ge(S["next_done"], it * 4 + 2 * m + 1)
                        act.copy(PX[m][:, :], NEXT[m][:, 0:P]).then_inc(S["px_copied"], 1)
                b = it - LN_ITER - 3
                if 0 <= b < BATCHES:
                    act.wait_ge(S["xt_done"], b + 1)
                    act.copy(XNT[:, b * BANK:(b + 1) * BANK], PRE[b % 2][:, :]).then_inc(S["xt_copied"], 1)
            for i in range(0, BATCHES, 2):
                act.wait_ge(S["u_done"], i + 1)
                act.copy(UT[:, i * BANK:(i + 1) * BANK], bank[4 + i % 4][:, :]).then_inc(S["u_copied_act"], 1)

            def one_pass(p, side, again):
                for n, j, g in slots():
                    if n < TILES:
                        act.wait_ge(w_ready[g], p * STEPS + j + 1)
                        act.activation(split(SQ[g][:, :]), state(j, g), ACT.Square).then_inc(sq_ready[g], 1)
                    m = n - 1
                    if side == "ffn" and 0 <= m < TILES:
                        act.wait_ge(S["ffn_done"], p * TILES + m + 1)
                        act.wait_ge(S["ffn_sum"], p * TILES + m + 1)
                        act.activation(FSQ[:, m % 2, :], SIDE[m % 2][:, 0:2 * FC], ACT.Square).then_inc(S["ffn_sq"], 1)
                    if side == "v" and 0 <= m < TILES:
                        act.wait_ge(S["v_done"], m + 1)
                        act.copy(VT[:, m * P:(m + 1) * P], SIDE[m % 2][:, 0:P]).then_inc(S["v_copied"], 1)
                    m = n - 2
                    if side == "ffn" and 0 <= m < TILES:
                        act.wait_ge(S["ffn_sum"], p * TILES + m + 1 + TWO)
                        act.wait_ge(S["xf_done"], p * TILES + m + 1)
                        act.activation(FR[:, m % 2, :], FS[:, m % 2, :], ACT.Sqrt).then_inc(S["ffn_root"], 1)
                    if n < TILES:
                        act.wait_ge(s_ready[g], p * STEPS + j + 1)
                        act.activation(RT[:, cols(j, g)], SUM[g][:, 0:P], ACT.Sqrt).then_inc(r_ready[g], 1)

            passes(act, one_pass)
            more_passes(act, one_pass)

        @block.vector
        def _(dve):
            dve.memset(ONES_WIDE[:, :], 1.0).then_inc(S["ones_ready"], 1)
            dve.sem_inc(S["ffn_sum"], TWO)
            dve.memset(MEAN[:, :], 1.0 / C).then_inc(S["consts_ready"], 1)
            dve.memset(EPS_MEAN[:, :], RMS_EPS / C).then_inc(S["consts_ready"], 1)
            dve.memset(EPS_LN[:, :], LN_EPS).then_inc(S["consts_ready"], 1)
            for g in range(GROUPS):
                dve.memset(EDGE[g][:, :, :], 0.0).then_inc(S["edge_init"], 1)
                dve.memset(EDGE_RI[g][:, :, :], 1.0).then_inc(S["edge_init"], 1)
            dve.wait_ge(S["ident_ready"], 2)
            dve.tensor_scalar(IDENT15[:, :], IDENT[:, :], 1.5, None, ALU.mult).then_inc(S["id15_ready"], 1)
            dve.wait_ge(S["wp_loaded"], 2 * 16)
            for m in range(2):
                dve.tensor_tensor_reduce(out=PP[m][:, :], in0=WP[m][:, :], in1=WP[m][:, :], scale=1.0, scalar=0.0,
                                         op0=ALU.mult, op1=ALU.add,
                                         accum_out=SSW[:, m:m + 1]).then_inc(S["polar_ss"], 1)
            dve.wait_ge(S["polar_nrm"], 1)
            dve.tensor_scalar(NRE[:, :], NRM[:, :], NORM_EPS, None, ALU.add).then_inc(S["polar_nre"], 1)
            dve.wait_ge(S["polar_nre"], 1)
            dve.reciprocal(NRI[:, :], NRE[:, :]).then_inc(S["polar_inv"], 1)
            dve.wait_ge(S["polar_inv"], 1)
            dve.wait_ge(S["wp_transposed"], 1)
            for m in range(2):
                dve.tensor_scalar(PX[m][:, :], WP[m][:, :], NRI[:, m:m + 1], None,
                                  ALU.mult).then_inc(S["px_copied"], 1)
            for m in range(2):
                dve.tensor_scalar(PXT[0][m][:, :], PRE[1][:, m * P:(m + 1) * P], NRI[:, m:m + 1], None,
                                  ALU.mult).then_inc(S["pxt_copied"], 1)

            def angles_sum():
                dve.wait_ge(S["ang_loaded"], 4 * 16)
                dve.tensor_tensor(ANG[:, :, :], ANG[:, :, :], NOISE[:, :, :], ALU.add).then_inc(S["ang_sum"], 1)
                dve.wait_ge(S["ang_sum"], 1)
                dve.tensor_scalar(ANG[:, 0, :], ANG[:, 0, :], math.pi / 2, None, ALU.add).then_inc(S["ang_sum"], 1)
                dve.wait_ge(S["ang_sum"], 2)
                dve.tensor_scalar(TURN[:, :, :], ANG[:, :, :], 0.5 / math.pi, ROUND, ALU.mult,
                                  ALU.add).then_inc(S["turn_a"], 1)

            def angles_turns():
                dve.wait_ge(S["turn_a"], 1)
                dve.tensor_scalar(TURN[:, :, :], TURN[:, :, :], ROUND, None, ALU.subtract).then_inc(S["turn_b"], 1)
                dve.wait_ge(S["turn_b"], 1)
                for n, part in enumerate((TWO_PI_A, TWO_PI_B, TWO_PI_C)):
                    dve.scalar_tensor_tensor(out=ANG[:, :, :], in0=TURN[:, :, :], scalar=-part, in1=ANG[:, :, :],
                                             op0=ALU.mult, op1=ALU.add).then_inc(S["turn_c"], 1)
                    dve.wait_ge(S["turn_c"], n + 1)
                dve.tensor_scalar(ANG[:, :, :], ANG[:, :, :], SIN_MAX, -SIN_MAX, ALU.min,
                                  ALU.max).then_inc(S["turn_d"], 1)

            def place_h0():
                dve.wait_ge(S["h0_loaded"], 16)
                dve.wait_ge(S["edge_init"], 2 * GROUPS)
                for g in range(GROUPS):
                    dve.tensor_scalar(EDGE[g][:, :, 0:1], EDGE[g][:, :, 0:1], H0[:, 0:1], None,
                                      ALU.add).then_inc(S["h0_placed"], 1)
                    dve.wait_ge(S["h0_placed"], g + 1)
                    dve.sem_inc(ri_ready[g], 1)

            def weights_transposed():
                dve.wait_ge(S["w_transposed"], 1)
                dve.tensor_copy(WVT[:, :], PRE[1][:, 2 * P:3 * P]).then_inc(S["wt_copied"], 1)
                dve.tensor_copy(WCT[:, :], PRE[1][:, 3 * P:4 * P]).then_inc(S["wt_copied"], 1)

            def row_stats(b, half):
                if 0 <= b < BATCHES:
                    dve.wait_ge(x_loaded[b * BT // GROUPS // QS], 16 * GROUPS)
                    for t in range(b * BT + half * BT // 2, b * BT + (half + 1) * BT // 2):
                        j, g = divmod(t, GROUPS)
                        dve.bn_stats(STATS[:, t, :], X[:, g, j, :]).then_inc(S["stats_done"], 1)

            def row_mean_var(b):
                if 0 <= b < BATCHES:
                    for t in range(b * BT, (b + 1) * BT):
                        dve.wait_ge(S["stats_done"], t + 1)
                        dve.bn_aggr(MV[:, t, :], STATS[:, t, :]).then_inc(S["mv_done"], 1)

            def row_rstd(b):
                if 0 <= b < BATCHES:
                    dve.wait_ge(S["sd_done"], b + 1)
                    dve.reciprocal(RSTD[:, b * BT:(b + 1) * BT],
                                   SD[:, b * BT:(b + 1) * BT]).then_inc(S["rstd_done"], 1)

            dve.wait_ge(S["id15_ready"], 1)
            for it in range(POLAR_ITERS):
                for m in range(2):
                    dve.wait_ge(S["gram_done"], it * 2 + m + 1)
                    dve.scalar_tensor_tensor(out=PP[m][:, :], in0=GRAM[m][:, 0:P], scalar=-0.5,
                                             in1=IDENT15[:, :], op0=ALU.mult, op1=ALU.add).then_inc(S["pp_done"], 1)
                if it == 0:
                    angles_sum()
                if it == 1:
                    weights_transposed()
                row_mean_var(it - LN_ITER - 1)
                row_stats(it - LN_ITER, 0)
                for m in range(2):
                    if it < SIN_ITERS:
                        dve.wait_ge(S["next_done"], it * 4 + 2 * m + 1)
                        dve.tensor_copy(PX[m][:, :], NEXT[m][:, 0:P]).then_inc(S["px_copied"], 1)
                    last = it == POLAR_ITERS - 1
                    dve.wait_ge(S["next_done"], it * 4 + (m + 1 if last else 2 * m + 2))
                    dve.tensor_copy(PXT[(it + 1) % 2][m][:, :], NEXTT[m][:, 0:P]).then_inc(S["pxt_copied"], 1)
                if it == 0:
                    angles_turns()
                if it == 1:
                    place_h0()
                row_rstd(it - LN_ITER - 1)
                row_stats(it - LN_ITER, 1)
            dve.wait_ge(S["mt_done"], 1)
            dve.tensor_copy(MT[:, :], GRAM[0][:, 0:P]).then_inc(S["mt_copied"], 1)
            for i in range(1, BATCHES, 2):
                dve.wait_ge(S["u_done"], i + 1)
                dve.tensor_copy(UT[:, i * BANK:(i + 1) * BANK], bank[4 + i % 4][:, :]).then_inc(S["u_copied_dve"], 1)

            def one_pass(p, side, again):
                for n, j, g in slots():
                    i = p * STEPS + j
                    if n < TILES and j == 0:
                        dve.wait_ge(ri_ready[g], p + 1)
                        dve.wait_ge(y_ready[g], i + 1)
                        dve.tensor_tensor(split(MIX[g][:, :]), split(Y[g][:, 0:P]), edge_old(EDGE_RI[g]),
                                          ALU.mult).then_inc(m_ready[g], 1)
                        dve.wait_ge(m_ready[g], i + 1)
                        dve.tensor_tensor(WT[:, cols(j, g)], MIX[g][:, :], UT[:, cols(j, g)],
                                          ALU.add).then_inc(w_ready[g], 1)
                    elif n < TILES:
                        dve.wait_ge(r_ready[g], i)
                        dve.tensor_tensor(MIX[g][:, :], UT[:, cols(j, g)], RT[:, cols(j - 1, g)],
                                          ALU.mult).then_inc(m_ready[g], 1)
                        dve.wait_ge(y_ready[g], i + 1)
                        dve.wait_ge(m_ready[g], i + 1)
                        if j == STEPS - 1:
                            dve.wait_ge(S["start_saved"], (p + 1) * GROUPS)
                        dve.tensor_tensor(state(j, g), split(MIX[g][:, :]), split(Y[g][:, 0:P]),
                                          ALU.add).then_inc(w_ready[g], 1)
                    m = n - 2
                    if side == "ffn" and 0 <= m < TILES:
                        dve.wait_ge(S["ffn_sq"], p * TILES + m + 1 + TWO)
                        dve.wait_ge(S["ffn_root"], p * TILES + m + 1)
                        dve.tensor_tensor(FS[:, m % 2, :], FSQ[:, m % 2, 0:FC], FSQ[:, m % 2, FC:2 * FC],
                                          ALU.add).then_inc(S["ffn_sum"], 1)
                    m = n - 3
                    if side == "out" and 0 <= m < TILES:
                        base = again * TILES
                        mj, mg = divmod(m, GROUPS)
                        dve.wait_ge(S["rinv_done"], base + m + 1)
                        dve.wait_ge(S["y_done"], base + m + 1)
                        dve.scalar_tensor_tensor(out=OUT[:, mg, mj, :], in0=SIDE[m % 2][:, 0:P],
                                                 scalar=RINV[:, m:m + 1], in1=XF[:, mg, mj, :],
                                                 op0=ALU.mult, op1=ALU.add).then_inc(S["out_done"], 1)
                    m = n - 2
                    if side == "out" and 0 <= m < TILES:
                        dve.wait_ge(S["rt_done"], again * TILES + m + 1)
                        dve.reciprocal(RINV[:, m:m + 1], ROW_R[m % 2][:, 0:1]).then_inc(S["rinv_done"], 1)
                    if j == STEPS - 1:
                        dve.wait_ge(r_ready[g], i + 1)
                        dve.reciprocal(edge_new(EDGE_RI[g]), split(RT[:, cols(j, g)])).then_inc(ri_ready[g], 1)

            dve.wait_ge(S["u_copied_act"], BATCHES // 2)
            dve.wait_ge(S["u_copied_dve"], BATCHES // 2)
            passes(dve, one_pass)
            for g in range(GROUPS):
                dve.wait_ge(ri_ready[g], WARM + 1)
                dve.tensor_tensor(split(DIFF[g][:, :]), edge_new(EDGE[g]), edge_new(EDGE_RI[g]),
                                  ALU.mult).then_inc(S["same_e"], 1)
            for g in range(GROUPS):
                dve.wait_ge(S["same_e"], g + 1)
                dve.tensor_tensor(DIFF[g][:, :], DIFF[g][:, :], START[g][:, :], ALU.subtract).then_inc(S["same_d"], 1)
            for g in range(GROUPS):
                dve.wait_ge(S["same_d"], g + 1)
                dve.tensor_tensor(DIFF[g][:, :], DIFF[g][:, :], DIFF[g][:, :], ALU.mult).then_inc(S["same_q"], 1)
            for g in range(GROUPS):
                dve.wait_ge(S["same_q"], g + 1)
                dve.tensor_scalar(DIFF[g][:, :], DIFF[g][:, :], TOL * TOL, None, ALU.is_le, ALU.add,
                                  accum_out=SAME[:, g:g + 1]).then_inc(S["same_done"], 1)
            dve.wait_ge(S["same_tot"], 1)
            dve.tensor_copy(SAMES[:, :], SUM[1][0:1, 0:GROUPS]).then_inc(S["same_row"], 1)
            dve.wait_ge(S["same_row"], 1)
            dve.tensor_tensor(SAMES[:, 0:1], SAMES[:, 0:1], SAMES[:, 1:2], ALU.add).then_inc(S["same_row"], 1)
            dve.wait_ge(S["same_row"], 2)
            dve.tensor_scalar(FLAG[:, 0:1], SAMES[:, 0:1], GROUPS * P * P - 0.5, None,
                              ALU.is_lt).then_inc(S["flag_ready"], 1)
            dve.wait_ge(S["stored"], 16 * XQ * GROUPS)
            more_passes(dve, one_pass)

        @block.tensor
        def _(pe):
            def keep_warm(n):
                for _ in range(n):
                    pe.matmul(bank[0][:, :], ONES_WIDE[:, 0:P], ONES_WIDE[:, :], start=True, stop=True)

            pe.wait_ge(S["ones_ready"], 1)
            keep_warm(3)
            pe.wait_ge(S["polar_ss"], 2)
            pe.matmul(PRE[0][:, 0:2], ONES[:, :], SSW[:, :], start=True, stop=True).then_inc(S["polar_tot"], 1)
            pe.wait_ge(S["ident_ready"], 2)
            for m in range(2):
                last = pe.transpose(PRE[1][:, m * P:(m + 1) * P], WP[m][:, :], IDENT[:, :])
            last.then_inc(S["wp_transposed"], 1)
            keep_warm(1)

            def transpose_tiles(b, half):
                if not 0 <= b < BATCHES:
                    return
                if b < 2:
                    pe.wait_ge(S["polar_nrm"], 1)
                    pe.wait_ge(S["wt_copied"], 2)
                else:
                    pe.wait_ge(S["xt_copied"], b - 1)
                for k in range(half * BT // 2, (half + 1) * BT // 2):
                    j, g = divmod(b * BT + k, GROUPS)
                    pe.wait_ge(S["xn_done"], b * BT + k + 1)
                    last = pe.transpose(PRE[b % 2][:, k * P:(k + 1) * P], XN[:, g, j, :], IDENT[:, :])
                if half:
                    last.then_inc(S["xt_done"], 1)

            for it in range(POLAR_ITERS):
                for m in range(2):
                    pe.wait_ge(S["px_copied"], it * 2 + m + 1)
                    pe.matmul(GRAM[m][:, 0:P], PX[m][:, :], PX[m][:, :], start=True,
                              stop=True).then_inc(S["gram_done"], 1)
                if it == 1:
                    pe.wait_ge(S["w_loaded"], 3 * 16)
                    pe.wait_ge(S["pxt_copied"], 2)
                    for i, w in enumerate((WV, WC)):
                        last = pe.transpose(PRE[1][:, (2 + i) * P:(3 + i) * P], w[:, :], IDENT[:, :])
                    last.then_inc(S["w_transposed"], 1)
                transpose_tiles(it - LN_ITER - 2, 0)
                for m in range(2):
                    pe.wait_ge(S["pxt_copied"], it * 2 + m + 1)
                    pe.wait_ge(S["pp_done"], it * 2 + m + 1)
                    if it < POLAR_ITERS - 1:
                        pe.matmul(NEXT[m][:, 0:P], PXT[it % 2][m][:, :], PP[m][:, :], start=True,
                                  stop=True).then_inc(S["next_done"], 1)
                    pe.matmul(NEXTT[m][:, 0:P], PP[m][:, :], PXT[it % 2][m][:, :], start=True,
                              stop=True).then_inc(S["next_done"], 1)
                transpose_tiles(it - LN_ITER - 2, 1)
            pe.wait_ge(S["pxt_copied"], POLAR_ITERS * 2 + 2)
            pe.matmul(GRAM[0][:, 0:P], WQ[:, :], OT[1][:, :], start=True, stop=True).then_inc(S["mt_done"], 1)
            for b in range(POLAR_ITERS - LN_ITER - 2, BATCHES):
                transpose_tiles(b, 0)
                transpose_tiles(b, 1)
            pe.wait_ge(S["mt_copied"], 1)
            pe.wait_ge(S["xt_copied"], BATCHES)
            for i in range(BATCHES):
                if i >= 4:
                    pe.wait_ge(S["u_copied_dve"] if i % 2 else S["u_copied_act"], i // 2 - 1)
                pe.matmul(bank[4 + i % 4][:, :], MT[:, :], XNT[:, i * BANK:(i + 1) * BANK], start=True,
                          stop=True).then_inc(S["u_done"], 1)
            pe.wait_ge(S["h0_placed"], GROUPS)
            for g in range(GROUPS):
                pe.matmul(split(Y[g][:, 0:P]), OT[0][:, :], edge_old(EDGE[g]), start=True,
                          stop=True).then_inc(y_ready[g], 1)
            pe.wait_ge(S["cs_done"], 2)
            pe.wait_ge(S["u_copied_act"], BATCHES // 2)
            pe.wait_ge(S["u_copied_dve"], BATCHES // 2)

            def one_pass(p, side, again):
                for n, j, g in slots():
                    if n < TILES:
                        pe.wait_ge(w_ready[g], p * STEPS + j + 1)
                        w = edge_old(EDGE[g]) if j == STEPS - 1 else state(j, g)
                        pe.matmul(split(Y[g][:, 0:P]), OT[0][:, :], w, start=True,
                                  stop=True).then_inc(y_ready[g], 1)
                        if j:
                            pe.wait_ge(q_ready[g], p * (STEPS - 1) + j)
                        q = Q[g][:, :] if j else ONES
                        pe.matmul(SUM[g][:, 0:P], EPS_MEAN[:, :], q, start=True, stop=False)
                        pe.wait_ge(sq_ready[g], p * STEPS + j + 1)
                        pe.matmul(SUM[g][:, 0:P], MEAN[:, :], SQ[g][:, :], start=False,
                                  stop=True).then_inc(s_ready[g], 1)
                        if side == "ffn":
                            pe.wait_ge(S["ffn_sq"], p * TILES + n + 1)
                            pe.matmul(SIDE[n % 2][:, 0:2 * FC].rearrange("r (h a c) -> r h a c", h=1, a=2),
                                      XNT[:, cols(j, g)], CS[:, bass.ds(p, 1), :, :],
                                      start=True, stop=True).then_inc(S["ffn_done"], 1)
                        if side == "v":
                            if n >= 2:
                                pe.wait_ge(S["v_copied"], n - 1)
                            else:
                                pe.wait_ge(S["ffn_sq"], FFN_PASSES * TILES + TWO)
                            pe.matmul(SIDE[n % 2][:, 0:P], WVT[:, :], XNT[:, cols(j, g)],
                                      start=True, stop=True).then_inc(S["v_done"], 1)
                    m = n - 1
                    if side == "out" and 0 <= m < TILES:
                        base = again * TILES
                        mj, mg = divmod(m, GROUPS)
                        pe.wait_ge(r_ready[mg], p * STEPS + mj + 1)
                        if base + m >= 2:
                            pe.wait_ge(S["rinv_done"], base + m - 1)
                        pe.matmul(ROW_R[m % 2][:, 0:1], RT[0:1, cols(mj, mg)], ONES_WIDE[0:1, 0:1],
                                  start=True, stop=True).then_inc(S["rt_done"], 1)
                        pe.wait_ge(S["pv_done"], base + m + 1)
                        if base + m >= 2:
                            pe.wait_ge(S["out_done"], base + m - 1)
                        else:
                            pe.wait_ge(S["v_copied"], TILES)
                        pe.matmul(SIDE[m % 2][:, 0:P], PV[:, m % 2, :], WCT[:, :],
                                  start=True, stop=True).then_inc(S["y_done"], 1)

            passes(pe, one_pass)
            pe.wait_ge(S["same_done"], GROUPS)
            pe.matmul(SUM[1][:, 0:GROUPS], ONES[:, :], SAME[:, :], start=True, stop=True).then_inc(S["same_tot"], 1)
            more_passes(pe, one_pass)


_INS = ['L0_attn_x', 'L0_attn_Wq', 'L0_attn_Wv', 'L0_attn_Wc', 'L0_attn_identity', 'L0_attn_W_lh', 'L0_attn_W_rh',
        'L0_ffn_theta', 'L0_ffn_phi', 'L0_ffn_theta_noise', 'L0_ffn_phi_noise']
_OUTS = [((8, 512, 128), 'float32')]


def kernel(**inputs):
    import numpy as _np
    import concourse.bacc as _bacc
    from concourse import mybir as _mybir
    from concourse.bass_utils import run_bass_kernel_spmd as _run

    nc = _bacc.Bacc("TRN2", target_bir_lowering=False, num_devices=1)
    arrays, args = {}, []
    for name in _INS:
        a = _np.ascontiguousarray(inputs[name])
        arrays[f"in_{name}_dram"] = a
        args.append(nc.dram_tensor(f"in_{name}_dram", a.shape, _mybir.dt.from_np(a.dtype), kind="ExternalInput").ap())
    for i, (shape, dtype) in enumerate(_OUTS):
        dt = _mybir.dt.from_np(_np.dtype(dtype))
        args.append(nc.dram_tensor(f"out_{i}_dram", shape, dt, kind="ExternalOutput").ap())
    bass_layer(nc, *args)
    r = _run(nc, [arrays], core_ids=[0])
    return r.results[0]["out_0_dram"]
```

```python
from contextlib import ExitStack
import math

import concourse.bass as bass
from concourse import mybir

ALU = mybir.AluOpType
ACT = mybir.ActivationFunctionType
F32 = mybir.dt.float32
I32 = mybir.dt.int32
BF16 = mybir.dt.bfloat16

LN_EPS = 1e-5
RMS_EPS = 1e-6
NORM_EPS = 1e-8
POLAR_ITERS = 12

STEPS = 16
FIRST = 6
WARM = 4
GUESSES = WARM - 1
TOL = 2e-5

TWO_PI_A = 6.28125
TWO_PI_B = 0.0019350051879882812
TWO_PI_C = 2.0 * math.pi - TWO_PI_A - TWO_PI_B
ROUND = 12582912.0
SIN_MAX = 3.1415925
LN_ITER = 1


def bass_layer(nc, x, Wq, Wv, Wc, identity, W_lh, W_rh, theta, phi, theta_noise, phi_noise, out):
    B, T, C = x.shape
    P = C
    NCHUNK = T // STEPS
    GROUPS = B * NCHUNK // P
    GB = B // GROUPS
    TILES = GROUPS * STEPS
    GW = GROUPS * P
    BANK = 512
    BT = BANK // P
    BATCHES = TILES // BT
    XQ = 4
    STORES = ((0, 4), (4, 8), (8, 12), (12, 14), (14, 16))
    QS = STEPS // XQ
    FFN_PASSES = 2
    FC = P // FFN_PASSES
    F0 = FIRST * GROUPS
    assert P == 128 and GROUPS == 2 and GB * NCHUNK == P and WARM == FFN_PASSES + 2 and F0 % BT == 0
    DVE_PROJ = [("u", t) for t in range(F0 + BT, TILES)] + [("u", t) for t in range(BT)]
    ACT_PROJ = [("u", t) for t in range(BT, F0)]
    V0 = TILES - F0 - len(ACT_PROJ)
    ACT_PROJ += [("v", t) for t in range(V0)]
    DVE_PROJ += [("v", t) for t in range(V0, TILES)]
    OUT_BATCHES = [(t, BT) for t in range(0, TILES - BT, BT)] + [(t, BT // 2) for t in range(TILES - BT, TILES, BT // 2)]
    BATCH_OF = [(b, t - first, n) for b, (first, n) in enumerate(OUT_BATCHES) for t in range(first, first + n)]

    ctx = ExitStack()
    with ctx:
        def sb(name, shape, dt=F32):
            return ctx.enter_context(nc.sbuf_tensor(name, shape, dt))

        def sem(name):
            return ctx.enter_context(nc.semaphore(name))

        bank = [ctx.enter_context(nc.psum_tensor(f"bank{i}", [P, BANK], F32)) for i in range(8)]

        X = sb("X", [P, GROUPS, STEPS, C])
        XN = sb("XN", [P, GROUPS, STEPS, C])
        XF = sb("XF", [P, GROUPS, STEPS, C])
        OUT = sb("OUT", [P, GROUPS, STEPS, C])
        XNT = sb("XNT", [P, STEPS * GW])
        UT = sb("UT", [P, STEPS * GW])
        VT = sb("VT", [P, STEPS * GW])
        WT = sb("WT", [P, STEPS * GW])
        RT = sb("RT", [P, STEPS * GW])
        EDGE = [sb(f"EDGE{g}", [P, GB, NCHUNK + 1]) for g in range(GROUPS)]
        EDGE_R = [sb(f"EDGE_R{g}", [P, GB, NCHUNK + 1]) for g in range(GROUPS)]
        EDGE_RI = [sb(f"EDGE_RI{g}", [P, GB, NCHUNK + 1]) for g in range(GROUPS)]
        START = [sb(f"START{g}", [P, P]) for g in range(GROUPS)]
        SQ = [sb(f"SQ{g}", [P, P]) for g in range(GROUPS)]
        MIX = [sb(f"MIX{g}", [P, P]) for g in range(GROUPS)]
        Q = [sb(f"Q{g}", [P, P]) for g in range(GROUPS)]
        SQ16 = [sb(f"SQ16_{g}", [P, P], BF16) for g in range(GROUPS)]
        Q16 = [sb(f"Q16_{g}", [P, P], BF16) for g in range(GROUPS)]
        MEAN16 = sb("MEAN16", [P, P], BF16)
        EPS_MEAN16 = sb("EPS_MEAN16", [P, P], BF16)
        ONES16 = sb("ONES16", [P, P], BF16)
        DIFF = [sb(f"DIFF{g}", [P, P]) for g in range(GROUPS)]
        STAYED = [sb(f"STAYED{g}", [P, P], BF16) for g in range(GROUPS)]
        STATS = sb("STATS", [P, TILES, 6])
        MV = sb("MV", [P, TILES, 2])
        SD = sb("SD", [P, TILES])
        RSTD = sb("RSTD", [P, TILES])
        SHIFT = sb("SHIFT", [P, TILES])
        WQ = sb("WQ", [P, P])
        WV = sb("WV", [P, P])
        WC = sb("WC", [P, P])
        WVT = sb("WVT", [P, P])
        WCT = sb("WCT", [P, P])
        MT = sb("MT", [P, P])
        WP = [sb(f"WP{m}", [P, P]) for m in range(2)]
        PX = [sb(f"PX{m}", [P, P]) for m in range(2)]
        PXT = [[sb(f"PXT{m}_{par}", [P, P]) for m in range(2)] for par in range(2)]
        PP = [sb(f"PP{m}", [P, P]) for m in range(2)]
        SSW = sb("SSW", [P, 2])
        NRM = sb("NRM", [P, 2])
        NRE = sb("NRE", [P, 2])
        NRI = sb("NRI", [P, 2])
        ROOT_OF_ONE = sb("ROOT_OF_ONE", [P, 2])
        H0 = sb("H0", [P, 1])
        IDENT = sb("IDENT", [P, P])
        IDENT15 = sb("IDENT15", [P, P])
        ONES_WIDE = sb("ONES_WIDE", [P, BANK])
        ONES = ONES_WIDE[:, 0:P]
        MEAN = sb("MEAN", [P, P])
        EPS_MEAN = sb("EPS_MEAN", [P, P])
        EPS_LN = sb("EPS_LN", [P, 1])
        ANG = sb("ANG", [P, 2, P])
        NOISE = sb("NOISE", [P, 2, P])
        TURN = sb("TURN", [P, 2, P])
        CS = sb("CS", [P, FFN_PASSES, 2, FC])
        RPACK = [sb(f"RPACK{i}", [P, P]) for i in range(2)]
        FSQ = sb("FSQ", [P, 2, 2 * FC])
        FS = sb("FS", [P, 2, FC])
        FR = sb("FR", [P, 2, FC])
        PV = sb("PV", [P, 2, P])
        RINV = sb("RINV", [P, TILES])
        SAMES = sb("SAMES", [1, P])
        SAME = sb("SAME", [1, 1])
        FLAG = sb("FLAG", [1, 2], I32)

        x_view = x.rearrange("(g b) (k j) c -> g (b k) j c", g=GROUPS, j=STEPS)
        out_view = out.rearrange("(g b) (k j) c -> g (b k) j c", g=GROUPS, j=STEPS)

        names = """wp_loaded w_loaded h0_loaded ang_loaded ones_ready consts_ready ident_ready id15_ready
            polar_ss polar_tot polar_nrm polar_inv polar_nre wp_transposed w_transposed wt_copied
            gram_done pp_done next_done px_transposed px_copied
            stats_done mv_done sd_done rstd_done shift_done xn_act xn_pool xt_done xt_copied xt_last_copied mt_done mt_copied
            u_done u_copied v_done v_copied ang_sum turn_a turn_b turn_c turn_d cs_done
            ffn_done ffn_sq ffn_sum ffn_root xf_done h0_placed edge_init start_saved
            pv_done pack_init pack_done rt_done rinv_done y_done out_done
            same_done same_tot same_row flag_ready stored""".split()
        S = {n: sem(n) for n in names}
        x_loaded = [sem(f"x_loaded{q}") for q in range(XQ)]
        w_ready = [sem(f"w_ready{g}") for g in range(GROUPS)]
        y_ready = [sem(f"y_ready{g}") for g in range(GROUPS)]
        m_ready = [sem(f"m_ready{g}") for g in range(GROUPS)]
        sq_ready = [sem(f"sq_ready{g}") for g in range(GROUPS)]
        q_ready = [sem(f"q_ready{g}") for g in range(GROUPS)]
        s_ready = [sem(f"s_ready{g}") for g in range(GROUPS)]
        r_ready = [sem(f"r_ready{g}") for g in range(GROUPS)]
        ri_ready = [sem(f"ri_ready{g}") for g in range(GROUPS)]

        pxt_copied = [sem(f"pxt_copied{m}") for m in range(2)]
        same = [sem(f"same{g}") for g in range(GROUPS)]

        OT = PXT[POLAR_ITERS % 2]
        GRAM, NEXT, NEXTT, PRE = bank[0:2], bank[2:4], bank[4:6], bank[6:8]
        Y, SUM, SIDE, ROW_R = bank[0:2], bank[2:4], bank[4:6], bank[6:8]

        def cols(j, g):
            return slice(j * GW + g * P, j * GW + (g + 1) * P)

        def split(ap):
            return ap.rearrange("p (b k) -> p b k", b=GB)

        def edge_new(buf):
            return buf[:, :, 1:NCHUNK + 1]

        def edge_old(buf):
            return buf[:, :, 0:NCHUNK]

        def r_of(j, g):
            return edge_new(EDGE_R[g]) if j == STEPS - 1 else split(RT[:, cols(j, g)])

        def r_before(j, g):
            return r_of(j - 1, g) if j else edge_old(EDGE_R[g])

        def state(j, g):
            return edge_new(EDGE[g]) if j == STEPS - 1 else split(WT[:, cols(j, g)])

        def guess_start(j, g):
            return split(UT[:, cols(j, g)])

        LAGS = 5
        START_AT = (3, 6)
        OUT_AT = (WARM - 1) * TILES

        def done(p, j):
            return p * STEPS + j - FIRST

        def passes(eng, one_pass):
            for p in range(WARM):
                one_pass(p, F0 if p == 0 else 0, p * TILES, 0)

        def more_passes(eng, one_pass):
            eng.wait_ge(S["flag_ready"], 1)
            more = eng.value_load(FLAG[0:1, 0:1], min_val=0, max_val=1)
            with eng.If(more > 0):
                with eng.Fori(WARM, NCHUNK - 1 + GUESSES) as p:
                    one_pass(p, 0, None, 0)
                one_pass(NCHUNK - 1 + GUESSES, 0, OUT_AT, 1)
            eng.end_ifs()

        def slots(n0, at):
            for n in range(n0, TILES + (LAGS if at == OUT_AT else 0)):
                yield n, *divmod(n, GROUPS)

        def side_slot(at, n):
            return -1 if at is None else at + n

        def guess(at):
            return at is not None and at < GUESSES * TILES

        def low(at):
            return at is not None and at < (GUESSES - 1) * TILES

        def renewed(at):
            return at is None or at > TILES

        def ri_count(p):
            return p - 1

        def ffn_item(slot, again):
            k = slot - TILES
            return k if 0 <= k < FFN_PASSES * TILES and not again else None

        def out_item(slot, again):
            m = slot - OUT_AT
            return (m, again * TILES + m) if 0 <= m < TILES else (None, None)

        def batch(m, again):
            b, i, n = BATCH_OF[m]
            return again * len(OUT_BATCHES) + b, i, n

        OUT_TILES = {}
        for first, size in OUT_BATCHES:
            for i in range(size):
                ready = first + size - 1 + 5
                OUT_TILES.setdefault(ready + (i if ready < TILES else i // 2), []).append(first + i)

        def y_bank(b):
            return (SIDE[0], SIDE[1], ROW_R[1])[b % 3]

        def proj(kind):
            return (MT, UT) if kind == "u" else (WVT, VT)

        block = ctx.enter_context(nc.Block())

        @block.sync
        def _(sp):
            sp.dma_start(WP[0][:, :], W_lh).then_inc(S["wp_loaded"], 16)
            for q in range(XQ):
                for g in range(GROUPS):
                    sp.dma_start(X[:, g, q * QS:(q + 1) * QS, :],
                                 x_view[g, :, q * QS:(q + 1) * QS, :]).then_inc(x_loaded[q], 16)
                if q == 0:
                    for src, dst in ((Wv, WV), (Wc, WC), (Wq, WQ)):
                        sp.dma_start(dst[:, :], src).then_inc(S["w_loaded"], 16)

            def store(t):
                for first, last in STORES:
                    sp.wait_ge(S["out_done"], t * TILES + last * GROUPS)
                    for g in range(GROUPS):
                        sp.dma_start(out_view[g, :, first:last, :],
                                     OUT[:, g, first:last, :]).then_inc(S["stored"], 16)
                sp.wait_ge(S["stored"], 16 * (t + 1) * len(STORES) * GROUPS)

            store(0)
            sp.wait_ge(S["flag_ready"], 1)
            more = sp.value_load(FLAG[0:1, 0:1], min_val=0, max_val=1)
            with sp.If(more > 0):
                store(1)
            sp.end_ifs()

        @block.gpsimd
        def _(pool):
            pool.memset(IDENT[:, :], 0.0).then_inc(S["ident_ready"], 1)
            pool.wait_ge(S["ident_ready"], 1)
            pool.affine_select(out=IDENT[:, :], in_=IDENT[:, :], compare_op=ALU.not_equal, fill=1.0, base=0,
                               pattern=[[-1, P]], channel_multiplier=1).then_inc(S["ident_ready"], 1)
            for src, dst in ((theta, ANG[:, 0, :]), (phi, ANG[:, 1, :]),
                             (theta_noise, NOISE[:, 0, :]), (phi_noise, NOISE[:, 1, :])):
                pool.dma_start(dst, src).then_inc(S["ang_loaded"], 16)
            pool.dma_start(H0[:, :], identity.rearrange("(c a) -> c a", a=1)).then_inc(S["h0_loaded"], 16)
            for b in range(BATCHES):
                pool.wait_ge(S["rstd_done"], b + 1)
                for t in (b * BT, b * BT + 3):
                    j, g = divmod(t, GROUPS)
                    pool.tensor_scalar(XN[:, g, j, :], X[:, g, j, :], MV[:, t, 0:1], RSTD[:, t:t + 1],
                                       ALU.subtract, ALU.mult).then_inc(S["xn_pool"], 1)

            def one_pass(p, n0, at, again):
                if at == OUT_AT:
                    pool.wait_ge(S["v_copied"], len(ACT_PROJ))
                    pool.wait_ge(S["u_copied"], len(DVE_PROJ) + 1)
                for n, j, g in slots(n0, at):
                    if n in START_AT and at == OUT_AT and not again:
                        e = START_AT.index(n)
                        pool.wait_ge(ri_ready[e], ri_count(p))
                        pool.tensor_tensor(split(START[e][:, :]), edge_new(EDGE[e]), edge_new(EDGE_RI[e]),
                                           ALU.mult).then_inc(S["start_saved"], 1)
                    k = ffn_item(side_slot(at, n) - 4, again)
                    if k is not None:
                        pool.wait_ge(S["ffn_root"], k + 1)
                        h, mj, mg = k // TILES, k % TILES // GROUPS, k % GROUPS
                        pool.tensor_tensor(XF[:, mg, mj, h * FC:(h + 1) * FC], X[:, mg, mj, h * FC:(h + 1) * FC],
                                           FR[:, k % 2, :], ALU.add).then_inc(S["xf_done"], 1)
                    m, k = out_item(side_slot(at, n), again)
                    if m is not None:
                        pool.wait_ge(w_ready[g], done(p, j) + 1)
                        if k >= 2:
                            pool.wait_ge(S["y_done"], k - 1)
                        pool.tensor_tensor(split(PV[:, n % 2, :]), split(VT[:, cols(j, g)]), state(j, g),
                                           ALU.mult).then_inc(S["pv_done"], 1)
                    if n < TILES:
                        pool.wait_ge(r_ready[g], done(p, j) + 1)
                        r = r_of(j, g) if j < STEPS - 1 or at == OUT_AT else edge_old(EDGE_R[g])
                        pool.tensor_tensor(split((Q16 if guess(at) else Q)[g][:, :]), r, r,
                                           ALU.mult).then_inc(q_ready[g], 1)

            passes(pool, one_pass)
            more_passes(pool, one_pass)

        @block.scalar
        def _(act):
            act.dma_start(WP[1][:, :], W_rh).then_inc(S["wp_loaded"], 16)
            act.wait_ge(S["ones_ready"], 1)
            act.activation(ROOT_OF_ONE[:, 0:1], ONES_WIDE[:, 0:1], ACT.Sqrt)
            act.wait_ge(S["polar_tot"], 1)
            act.activation(NRM[:, :], PRE[0][:, 0:2], ACT.Sqrt).then_inc(S["polar_nrm"], 1)
            def rows_normalised(b, k):
                if 0 <= b < BATCHES:
                    act.wait_ge(S["shift_done"], b + 1)
                    t = b * BT + k
                    j, g = divmod(t, GROUPS)
                    act.activation(XN[:, g, j, :], X[:, g, j, :], ACT.Identity, bias=SHIFT[:, t:t + 1],
                                   scale=RSTD[:, t:t + 1]).then_inc(S["xn_act"], 1)

            for it in range(POLAR_ITERS):
                if 0 < it < POLAR_ITERS - 1:
                    act.wait_ge(S["px_transposed"], it * 2)
                    act.copy(PXT[it % 2][1][:, :], NEXTT[1][:, 0:P]).then_inc(pxt_copied[1], 1)
                if it < POLAR_ITERS - 1:
                    rows_normalised(it - LN_ITER - 3, 2)
                    for m in range(2):
                        act.wait_ge(S["next_done"], it * 2 + m + 1)
                        act.copy(PX[m][:, :], NEXT[m][:, 0:P]).then_inc(S["px_copied"], 1)
                b = it - LN_ITER - 1
                if 0 <= b < BATCHES:
                    act.wait_ge(S["mv_done"], (b + 1) * BT)
                    act.activation(SD[:, b * BT:(b + 1) * BT], MV[:, b * BT:(b + 1) * BT, 1:2], ACT.Sqrt,
                                   bias=EPS_LN[:, :]).then_inc(S["sd_done"], 1)
                rows_normalised(it - LN_ITER - 2, 1)
                if it == POLAR_ITERS - 2:
                    rows_normalised(it - LN_ITER - 2, 2)
                b = it - LN_ITER - 3
                if 0 <= b < BATCHES - 1:
                    act.wait_ge(S["xt_done"], b + 1)
                    act.copy(XNT[:, b * BANK:(b + 1) * BANK], PRE[b % 2][:, :]).then_inc(S["xt_copied"], 1)
                if it == POLAR_ITERS - 2:
                    act.wait_ge(S["turn_d"], 1)
                    act.activation(CS[:, :, :, :], ANG[:, :, :].rearrange("p a (h c) -> p h a c", h=FFN_PASSES),
                                   ACT.Sin).then_inc(S["cs_done"], 1)
            act.activation(ROOT_OF_ONE[:, 1:2], ONES_WIDE[:, 0:1], ACT.Sqrt)

            def side_work(p, slot, again):
                k = slot - 1 - F0
                if 0 <= k < len(ACT_PROJ):
                    kind, t = ACT_PROJ[k]
                    act.wait_ge(S["v_done"], k + 1)
                    act.copy(proj(kind)[1][:, t * P:(t + 1) * P], SIDE[k % 2][:, 0:P]).then_inc(S["v_copied"], 1)
                k = ffn_item(slot - 1, again)
                if k is not None:
                    act.wait_ge(S["ffn_done"], k + 1)
                    if k >= 2:
                        act.wait_ge(S["ffn_sum"], k - 1)
                    act.activation(FSQ[:, k % 2, :], SIDE[k % 2][:, 0:2 * FC], ACT.Square).then_inc(S["ffn_sq"], 1)
                k = ffn_item(slot - 3, again)
                if k is not None:
                    act.wait_ge(S["ffn_sum"], k + 1)
                    if k >= 2:
                        act.wait_ge(S["xf_done"], k - 1)
                    act.activation(FR[:, k % 2, :], FS[:, k % 2, :], ACT.Sqrt).then_inc(S["ffn_root"], 1)
                m, k = out_item(slot - 1, again)
                if m is not None:
                    b, i, _ = batch(m, again)
                    mj, mg = divmod(m, GROUPS)
                    act.wait_ge(r_ready[mg], done(p, mj) + 1)
                    if i == 0 and b >= 2:
                        act.wait_ge(S["rt_done"], b - 1)
                    act.copy(split(RPACK[b % 2][32 * i:32 * i + 1, :]),
                             r_of(mj, mg)[32 * i:32 * i + 1, :, :]).then_inc(S["pack_done"], 1)

            def one_pass(p, n0, at, again):
                for n, j, g in slots(n0, at):
                    if n < TILES:
                        act.wait_ge(w_ready[g], done(p, j) + 1)
                        act.activation(split((SQ16 if low(at) else SQ)[g][:, :]),
                                       guess_start(j, g) if at == 0 and j == FIRST else state(j, g),
                                       ACT.Square).then_inc(sq_ready[g], 1)
                    side_work(p, side_slot(at, n), again)
                    if n < TILES:
                        act.wait_ge(s_ready[g], done(p, j) + 1)
                        act.activation(r_of(j, g), split(SUM[g][:, 0:P]), ACT.Sqrt).then_inc(r_ready[g], 1)

            passes(act, one_pass)
            more_passes(act, one_pass)

        @block.vector
        def _(dve):
            dve.memset(ONES_WIDE[:, :], 1.0).then_inc(S["ones_ready"], 1)
            dve.memset(MEAN[:, :], 1.0 / C).then_inc(S["consts_ready"], 1)
            dve.memset(EPS_MEAN[:, :], RMS_EPS / C).then_inc(S["consts_ready"], 1)
            dve.memset(EPS_LN[:, :], LN_EPS).then_inc(S["consts_ready"], 1)
            dve.memset(MEAN16[:, :], 1.0 / C).then_inc(S["consts_ready"], 1)
            dve.memset(EPS_MEAN16[:, :], RMS_EPS / C).then_inc(S["consts_ready"], 1)
            dve.memset(ONES16[:, :], 1.0).then_inc(S["consts_ready"], 1)
            for g in range(GROUPS):
                dve.memset(EDGE[g][:, :, :], 0.0).then_inc(S["edge_init"], 1)
                dve.memset(EDGE_R[g][:, :, :], 1.0).then_inc(S["edge_init"], 1)
                dve.memset(EDGE_RI[g][:, :, :], 1.0).then_inc(S["edge_init"], 1)
                dve.memset(RPACK[g][:, :], 0.0).then_inc(S["pack_init"], 1)
            dve.wait_ge(S["ident_ready"], 2)
            dve.tensor_scalar(IDENT15[:, :], IDENT[:, :], 1.5, None, ALU.mult).then_inc(S["id15_ready"], 1)
            dve.wait_ge(S["wp_loaded"], 2 * 16)
            for m in range(2):
                dve.tensor_tensor_reduce(out=PP[m][:, :], in0=WP[m][:, :], in1=WP[m][:, :], scale=1.0, scalar=0.0,
                                         op0=ALU.mult, op1=ALU.add,
                                         accum_out=SSW[:, m:m + 1]).then_inc(S["polar_ss"], 1)
            dve.wait_ge(S["polar_nrm"], 1)
            dve.tensor_scalar(NRE[:, :], NRM[:, :], NORM_EPS, None, ALU.add).then_inc(S["polar_nre"], 1)
            dve.wait_ge(S["polar_nre"], 1)
            dve.reciprocal(NRI[:, :], NRE[:, :]).then_inc(S["polar_inv"], 1)
            dve.wait_ge(S["polar_inv"], 1)
            dve.wait_ge(S["wp_transposed"], 1)
            for m in range(2):
                dve.tensor_scalar(PX[m][:, :], WP[m][:, :], NRI[:, m:m + 1], None,
                                  ALU.mult).then_inc(S["px_copied"], 1)
            for m in range(2):
                dve.tensor_scalar(PXT[0][m][:, :], PRE[1][:, m * P:(m + 1) * P], NRI[:, m:m + 1], None,
                                  ALU.mult).then_inc(pxt_copied[m], 1)

            def angles_sum():
                dve.wait_ge(S["ang_loaded"], 4 * 16)
                dve.tensor_tensor(ANG[:, :, :], ANG[:, :, :], NOISE[:, :, :], ALU.add).then_inc(S["ang_sum"], 1)

            def angles_shifted():
                dve.wait_ge(S["ang_sum"], 1)
                dve.tensor_scalar(ANG[:, 0, :], ANG[:, 0, :], math.pi / 2, None, ALU.add).then_inc(S["ang_sum"], 1)

            def turns():
                dve.wait_ge(S["ang_sum"], 2)
                dve.tensor_scalar(TURN[:, :, :], ANG[:, :, :], 0.5 / math.pi, ROUND, ALU.mult,
                                  ALU.add).then_inc(S["turn_a"], 1)

            def turns_rounded():
                dve.wait_ge(S["turn_a"], 1)
                dve.tensor_scalar(TURN[:, :, :], TURN[:, :, :], ROUND, None, ALU.subtract).then_inc(S["turn_b"], 1)

            def turns_off(n, part):
                dve.wait_ge(S["turn_b"], 1)
                if n:
                    dve.wait_ge(S["turn_c"], n)
                dve.scalar_tensor_tensor(out=ANG[:, :, :], in0=TURN[:, :, :], scalar=-part, in1=ANG[:, :, :],
                                         op0=ALU.mult, op1=ALU.add).then_inc(S["turn_c"], 1)

            def angles_clipped():
                dve.wait_ge(S["turn_c"], 3)
                dve.tensor_scalar(ANG[:, :, :], ANG[:, :, :], SIN_MAX, -SIN_MAX, ALU.min,
                                  ALU.max).then_inc(S["turn_d"], 1)

            def place_h0():
                dve.wait_ge(S["h0_loaded"], 16)
                dve.wait_ge(S["edge_init"], 3 * GROUPS)
                for g in range(GROUPS):
                    dve.tensor_scalar(EDGE[g][:, :, 0:1], EDGE[g][:, :, 0:1], H0[:, 0:1], None,
                                      ALU.add).then_inc(S["h0_placed"], 1)

            def weights_transposed():
                dve.wait_ge(S["w_transposed"], 1)
                dve.tensor_copy(WVT[:, :], PRE[1][:, 2 * P:3 * P]).then_inc(S["wt_copied"], 1)
                dve.tensor_copy(WCT[:, :], PRE[1][:, 3 * P:4 * P]).then_inc(S["wt_copied"], 1)

            def row_stats(b, tiles):
                if 0 <= b < BATCHES:
                    dve.wait_ge(x_loaded[b * BT // GROUPS // QS], 16 * GROUPS)
                    for t in range(b * BT, (b + 1) * BT)[tiles]:
                        j, g = divmod(t, GROUPS)
                        dve.bn_stats(STATS[:, t, :], X[:, g, j, :]).then_inc(S["stats_done"], 1)

            def row_mean_var(b):
                if 0 <= b < BATCHES:
                    for t in range(b * BT, (b + 1) * BT):
                        dve.wait_ge(S["stats_done"], t + 1)
                        dve.bn_aggr(MV[:, t, :], STATS[:, t, :]).then_inc(S["mv_done"], 1)

            def row_rstd(b):
                if 0 <= b < BATCHES:
                    dve.wait_ge(S["sd_done"], b + 1)
                    dve.reciprocal(RSTD[:, b * BT:(b + 1) * BT],
                                   SD[:, b * BT:(b + 1) * BT]).then_inc(S["rstd_done"], 1)

            def rows_normalised(b):
                if 0 <= b < BATCHES:
                    dve.wait_ge(S["rstd_done"], b + 1)
                    t = b * BT + 1
                    dve.scalar_tensor_tensor(out=SHIFT[:, t:t + 2], in0=MV[:, t:t + 2, 0], scalar=-1.0,
                                             in1=RSTD[:, t:t + 2], op0=ALU.mult,
                                             op1=ALU.mult).then_inc(S["shift_done"], 1)

            dve.wait_ge(S["id15_ready"], 1)
            for it in range(POLAR_ITERS):
                for m in range(2):
                    dve.wait_ge(S["gram_done"], it * 2 + m + 1)
                    dve.scalar_tensor_tensor(out=PP[m][:, :], in0=GRAM[m][:, 0:P], scalar=-0.5,
                                             in1=IDENT15[:, :], op0=ALU.mult, op1=ALU.add).then_inc(S["pp_done"], 1)
                    if it and m == 0 or it == POLAR_ITERS - 1:
                        dve.wait_ge(S["px_transposed"], it * 2 - 1 + m)
                        dve.tensor_copy(PXT[it % 2][m][:, :], NEXTT[m][:, 0:P]).then_inc(pxt_copied[m], 1)
                if it == 1:
                    weights_transposed()
                row_rstd(it - LN_ITER - 2)
                row_mean_var(it - LN_ITER - 1)
                rows_normalised(it - LN_ITER - 2)
                if it == 2:
                    angles_sum()
                if it == POLAR_ITERS - 4:
                    place_h0()
                if it == POLAR_ITERS - 3:
                    turns_off(0, TWO_PI_A)
                row_stats(it - LN_ITER, slice(0, BT))
                if it == 2:
                    angles_shifted()
                if it == 3:
                    turns()
                if it == POLAR_ITERS - 4:
                    turns_rounded()
                if it == POLAR_ITERS - 3:
                    turns_off(1, TWO_PI_B)
                if it == POLAR_ITERS - 2:
                    turns_off(2, TWO_PI_C)
                    angles_clipped()
            for m in range(2):
                dve.wait_ge(S["next_done"], (POLAR_ITERS - 1) * 2 + m + 1)
                dve.tensor_copy(OT[m][:, :], NEXTT[m][:, 0:P]).then_inc(pxt_copied[m], 1)
            dve.wait_ge(S["mt_done"], 1)
            dve.tensor_copy(MT[:, :], GRAM[0][:, 0:P]).then_inc(S["mt_copied"], 1)
            dve.wait_ge(S["u_done"], 1)
            for g in range(GROUPS):
                dve.tensor_copy(UT[:, cols(FIRST, g)], ROW_R[0][:, g * P:(g + 1) * P]).then_inc(w_ready[g], 1)
            dve.tensor_copy(UT[:, (F0 + GROUPS) * P:(F0 + BT) * P],
                            ROW_R[0][:, GROUPS * P:BT * P]).then_inc(S["u_copied"], 1)
            dve.wait_ge(S["xt_done"], BATCHES)
            dve.tensor_copy(XNT[:, (BATCHES - 1) * BANK:],
                            PRE[(BATCHES - 1) % 2][:, :]).then_inc(S["xt_last_copied"], 1)

            def edge_inverse(p, g):
                dve.wait_ge(r_ready[g], done(p, 0))
                dve.reciprocal(edge_new(EDGE_RI[g]), edge_new(EDGE_R[g])).then_inc(ri_ready[g], 1)

            def check_stage(p, g, stage):
                if stage == 0:
                    dve.wait_ge(r_ready[g], done(p, STEPS))
                    dve.wait_ge(S["start_saved"], g + 1)
                    dve.tensor_tensor(split(DIFF[g][:, :]), split(START[g][:, :]), edge_new(EDGE_R[g]),
                                      ALU.mult).then_inc(same[g], 1)
                if stage == 1:
                    dve.wait_ge(same[g], 1)
                    dve.wait_ge(w_ready[g], done(p, STEPS))
                    dve.tensor_tensor(split(DIFF[g][:, :]), edge_new(EDGE[g]), split(DIFF[g][:, :]),
                                      ALU.subtract).then_inc(same[g], 1)
                if stage == 2:
                    dve.wait_ge(same[g], 2)
                    dve.tensor_tensor(DIFF[g][:, :], DIFF[g][:, :], DIFF[g][:, :], ALU.mult).then_inc(same[g], 1)
                if stage == 3:
                    dve.wait_ge(same[g], 3)
                    dve.wait_ge(q_ready[g], done(p, STEPS))
                    dve.scalar_tensor_tensor(out=STAYED[g][:, :], in0=Q[g][:, :], scalar=TOL * TOL, in1=DIFF[g][:, :],
                                             op0=ALU.mult, op1=ALU.is_gt).then_inc(S["same_done"], 1)

            def side_work(slot, again):
                k = slot - 2 - F0
                if 0 <= k < len(DVE_PROJ):
                    kind, t = DVE_PROJ[k]
                    dve.wait_ge(S["u_done"], k + 2)
                    dve.tensor_copy(proj(kind)[1][:, t * P:(t + 1) * P],
                                    ROW_R[(k + 1) % 2][:, 0:P]).then_inc(S["u_copied"], 1)
                for t in OUT_TILES.get(slot - OUT_AT, ()):
                    count, i, size = batch(t, again)
                    tj, tg = divmod(t, GROUPS)
                    if i == 0:
                        dve.wait_ge(S["rinv_done"], count + 1)
                        dve.wait_ge(S["y_done"], again * TILES + t + size)
                    dve.scalar_tensor_tensor(out=OUT[:, tg, tj, :], in0=y_bank(count)[:, i * P:(i + 1) * P],
                                             scalar=RINV[:, t:t + 1], in1=XF[:, tg, tj, :],
                                             op0=ALU.mult, op1=ALU.add).then_inc(S["out_done"], 1)
                m, _ = out_item(slot - 4, again)
                if m is not None:
                    count, i, size = batch(m, again)
                    if i == size - 1:
                        dve.wait_ge(S["rt_done"], count + 1)
                        dve.reciprocal(RINV[:, m + 1 - size:m + 1], ROW_R[0][:, 0:size]).then_inc(S["rinv_done"], 1)

            def ffn_sum(slot, again):
                k = ffn_item(slot - 2, again)
                if k is not None:
                    dve.wait_ge(S["ffn_sq"], k + 1)
                    if k >= 2:
                        dve.wait_ge(S["ffn_root"], k - 1)
                    dve.tensor_tensor(FS[:, k % 2, :], FSQ[:, k % 2, 0:FC], FSQ[:, k % 2, FC:2 * FC],
                                      ALU.add).then_inc(S["ffn_sum"], 1)

            def u_ready(p, m):
                for pipe, copied, before in ((DVE_PROJ, "u_copied", 1), (ACT_PROJ, "v_copied", 0)):
                    if ("u", m) in pipe:
                        if (m >= F0) == (p == 0):
                            dve.wait_ge(S[copied], pipe.index(("u", m)) + 1 + before)
                        return
                dve.wait_ge(S["u_copied"], 1)

            def one_pass(p, n0, at, again):
                for n, j, g in slots(n0, at):
                    if at == OUT_AT and not again:
                        if n - TILES in (1, 2):
                            check_stage(p, 0, n - TILES - 1)
                    i = done(p, j)
                    if at in (0, TILES) and n < TILES:
                        u_ready(p, n)
                    if n >= TILES or (at == 0 and j == FIRST):
                        side_work(side_slot(at, n), again)
                    elif j == 0 and renewed(at):
                        edge_inverse(p, g)
                        dve.wait_ge(ri_ready[g], ri_count(p))
                        dve.wait_ge(y_ready[g], i)
                        dve.tensor_tensor(split(MIX[g][:, :]), split(Y[g][:, 0:P]), edge_old(EDGE_RI[g]),
                                          ALU.mult).then_inc(m_ready[g], 1)
                        side_work(side_slot(at, n), again)
                        dve.wait_ge(m_ready[g], i)
                        dve.tensor_tensor(WT[:, cols(j, g)], MIX[g][:, :], UT[:, cols(j, g)],
                                          ALU.add).then_inc(w_ready[g], 1)
                    else:
                        dve.wait_ge(r_ready[g], i)
                        dve.tensor_tensor(split(MIX[g][:, :]), split(UT[:, cols(j, g)]), r_before(j, g),
                                          ALU.mult).then_inc(m_ready[g], 1)
                        side_work(side_slot(at, n), again)
                        dve.wait_ge(y_ready[g], i)
                        dve.wait_ge(m_ready[g], i)
                        if j == STEPS - 1 and at == OUT_AT and not again:
                            dve.wait_ge(S["start_saved"], GROUPS)
                        dve.tensor_tensor(state(j, g), split(MIX[g][:, :]), split(Y[g][:, 0:P]),
                                          ALU.add).then_inc(w_ready[g], 1)
                    ffn_sum(side_slot(at, n), again)

            passes(dve, one_pass)
            for e, stage in ((1, 0), (0, 2), (1, 1), (0, 3), (1, 2), (1, 3)):
                check_stage(WARM - 1, e, stage)
            dve.wait_ge(S["same_tot"], 1)
            dve.tensor_scalar(SAMES[:, :], SUM[1][0:1, 0:P], GROUPS * P - 0.5, None, ALU.is_ge, ALU.add,
                              accum_out=SAME[:, :]).then_inc(S["same_row"], 1)
            dve.wait_ge(S["same_row"], 1)
            dve.tensor_scalar(FLAG[:, 0:1], SAME[:, :], P - 0.5, None, ALU.is_lt).then_inc(S["flag_ready"], 1)
            dve.wait_ge(S["stored"], 16 * len(STORES) * GROUPS)
            more_passes(dve, one_pass)

        @block.tensor
        def _(pe):
            def keep_warm(n):
                for _ in range(n):
                    pe.matmul(bank[1][:, 0:P], ONES[:, :], ONES[:, :], start=True, stop=True)

            pe.wait_ge(S["ones_ready"], 1)
            keep_warm(6)
            pe.wait_ge(S["polar_ss"], 2)
            pe.matmul(PRE[0][:, 0:2], ONES[:, :], SSW[:, :], start=True, stop=True).then_inc(S["polar_tot"], 1)
            pe.wait_ge(S["ident_ready"], 2)
            for m in range(2):
                last = pe.transpose(PRE[1][:, m * P:(m + 1) * P], WP[m][:, :], IDENT[:, :])
            last.then_inc(S["wp_transposed"], 1)
            keep_warm(2)

            def transpose_tiles(b, half):
                if not 0 <= b < BATCHES:
                    return
                if b < 2:
                    pe.wait_ge(S["polar_nrm"], 1)
                    pe.wait_ge(S["wt_copied"], 2)
                else:
                    pe.wait_ge(S["xt_copied"], b - 1)
                for k in range(half * BT // 2, (half + 1) * BT // 2):
                    j, g = divmod(b * BT + k, GROUPS)
                    pe.wait_ge(*((S["xn_pool"], 2 * b + 1), (S["xn_act"], 2 * b + 1),
                                 (S["xn_act"], 2 * b + 2), (S["xn_pool"], 2 * b + 2))[k])
                    last = pe.transpose(PRE[b % 2][:, k * P:(k + 1) * P], XN[:, g, j, :], IDENT[:, :])
                if half:
                    last.then_inc(S["xt_done"], 1)

            for it in range(POLAR_ITERS):
                for m in range(2):
                    pe.wait_ge(S["px_copied"], it * 2 + m + 1)
                    pe.matmul(GRAM[m][:, 0:P], PX[m][:, :], PX[m][:, :], start=True,
                              stop=True).then_inc(S["gram_done"], 1)
                if it:
                    for m in range(2):
                        pe.transpose(NEXTT[m][:, 0:P], PX[m][:, :], IDENT[:, :]).then_inc(S["px_transposed"], 1)
                if it == 1:
                    pe.wait_ge(S["w_loaded"], 3 * 16)
                    for i, w in enumerate((WV, WC)):
                        last = pe.transpose(PRE[1][:, (2 + i) * P:(3 + i) * P], w[:, :], IDENT[:, :])
                    last.then_inc(S["w_transposed"], 1)
                for m in range(2):
                    pe.wait_ge(pxt_copied[m], it + 1)
                    pe.wait_ge(S["pp_done"], it * 2 + m + 1)
                    if it < POLAR_ITERS - 1:
                        pe.matmul(NEXT[m][:, 0:P], PXT[it % 2][m][:, :], PP[m][:, :], start=True,
                                  stop=True).then_inc(S["next_done"], 1)
                    else:
                        pe.matmul(NEXTT[m][:, 0:P], PP[m][:, :], PXT[it % 2][m][:, :], start=True,
                                  stop=True).then_inc(S["next_done"], 1)
                if it < POLAR_ITERS - 1:
                    transpose_tiles(it - LN_ITER - 3, 0)
                    transpose_tiles(it - LN_ITER - 3, 1)
            for m in range(2):
                pe.wait_ge(pxt_copied[m], POLAR_ITERS + 1)
            pe.matmul(GRAM[0][:, 0:P], WQ[:, :], OT[1][:, :], start=True, stop=True).then_inc(S["mt_done"], 1)
            for b in range(POLAR_ITERS - LN_ITER - 4, BATCHES):
                transpose_tiles(b, 0)
                transpose_tiles(b, 1)
            pe.wait_ge(S["mt_copied"], 1)
            pe.wait_ge(S["xt_copied"], BATCHES - 1)
            pe.matmul(ROW_R[0][:, :], MT[:, :], XNT[:, F0 * P:F0 * P + BANK], start=True, stop=True).then_inc(S["u_done"], 1)
            pe.wait_ge(S["cs_done"], 1)
            pe.wait_ge(S["h0_placed"], GROUPS)

            def side_work(p, slot, again):
                k = slot - F0
                if 0 <= k < len(ACT_PROJ):
                    kind, t = ACT_PROJ[k]
                    if k >= 2:
                        pe.wait_ge(S["v_copied"], k - 1)
                    pe.matmul(SIDE[k % 2][:, 0:P], proj(kind)[0][:, :], XNT[:, t * P:(t + 1) * P],
                              start=True, stop=True).then_inc(S["v_done"], 1)
                if 0 <= k < len(DVE_PROJ):
                    kind, t = DVE_PROJ[k]
                    if k == 0:
                        pe.wait_ge(S["xt_last_copied"], 1)
                    if k >= 1:
                        pe.wait_ge(S["u_copied"], k)
                    pe.matmul(ROW_R[(k + 1) % 2][:, 0:P], proj(kind)[0][:, :], XNT[:, t * P:(t + 1) * P],
                              start=True, stop=True).then_inc(S["u_done"], 1)
                k = ffn_item(slot, again)
                if k is not None:
                    h, m = divmod(k, TILES)
                    if k == 0:
                        pe.wait_ge(S["v_copied"], len(ACT_PROJ))
                    if k >= 2:
                        pe.wait_ge(S["ffn_sq"], k - 1)
                    pe.matmul(SIDE[k % 2][:, 0:2 * FC].rearrange("r (a c) -> r a c", a=2),
                              XNT[:, m * P:(m + 1) * P], CS[:, h, :, :],
                              start=True, stop=True).then_inc(S["ffn_done"], 1)
                m, k = out_item(slot - 1, again)
                if m is not None:
                    b, i, _ = batch(m, again)
                    if k == 0:
                        pe.wait_ge(S["ffn_sq"], FFN_PASSES * TILES)
                        pe.wait_ge(S["u_copied"], len(DVE_PROJ) + 1)
                    if i == 0 and b >= 3:
                        first, size = OUT_BATCHES[(b - 3) % len(OUT_BATCHES)]
                        pe.wait_ge(S["out_done"], (b - 3) // len(OUT_BATCHES) * TILES + first + size)
                    pe.wait_ge(S["pv_done"], k + 1)
                    pe.matmul(y_bank(b)[:, i * P:(i + 1) * P], PV[:, m % 2, :], WCT[:, :],
                              start=True, stop=True).then_inc(S["y_done"], 1)
                m, k = out_item(slot - 2, again)
                if m is not None:
                    b, i, size = batch(m, again)
                    if i == size - 1:
                        pe.wait_ge(S["pack_init"], 2)
                        pe.wait_ge(S["pack_done"], k + 1)
                        if b:
                            pe.wait_ge(S["rinv_done"], b)
                        pe.matmul(ROW_R[0][:, 0:size], RPACK[b % 2][:, :], IDENT[:, 0:32 * size:32],
                                  start=True, stop=True).then_inc(S["rt_done"], 1)

            def one_pass(p, n0, at, again):
                for n, j, g in slots(n0, at):
                    if n < TILES:
                        pe.wait_ge(w_ready[g], done(p, j) + 1)
                        start = at == 0 and j == FIRST
                        w = guess_start(j, g) if start else edge_old(EDGE[g]) if j == STEPS - 1 else state(j, g)
                        pe.matmul(split(Y[g][:, 0:P]), OT[0][:, :], w, start=True,
                                  stop=True).then_inc(y_ready[g], 1)
                        ones = start or (j == 0 and renewed(at))
                        if not start:
                            pe.wait_ge(q_ready[g], done(p, j))
                        if guess(at):
                            q, eps_mean = ONES16[:, :] if ones else Q16[g][:, :], EPS_MEAN16
                        else:
                            q, eps_mean = ONES if ones else Q[g][:, :], EPS_MEAN
                        sq, mean = (SQ16[g], MEAN16) if low(at) else (SQ[g], MEAN)
                        pe.matmul(SUM[g][:, 0:P], eps_mean[:, :], q, start=True, stop=False)
                        pe.wait_ge(sq_ready[g], done(p, j) + 1)
                        pe.matmul(SUM[g][:, 0:P], mean[:, :], sq[:, :], start=False,
                                  stop=True).then_inc(s_ready[g], 1)
                    side_work(p, side_slot(at, n), again)

            passes(pe, one_pass)
            pe.wait_ge(S["same_done"], GROUPS)
            pe.matmul(SUM[1][:, 0:P], ONES16[:, :], STAYED[0][:, :], start=True, stop=False)
            pe.matmul(SUM[1][:, 0:P], ONES16[:, :], STAYED[1][:, :], start=False, stop=True).then_inc(S["same_tot"], 1)
            more_passes(pe, one_pass)


_INS = ['L0_attn_x', 'L0_attn_Wq', 'L0_attn_Wv', 'L0_attn_Wc', 'L0_attn_identity', 'L0_attn_W_lh', 'L0_attn_W_rh',
        'L0_ffn_theta', 'L0_ffn_phi', 'L0_ffn_theta_noise', 'L0_ffn_phi_noise']
_OUTS = [((8, 512, 128), 'float32')]


def kernel(**inputs):
    import numpy as _np
    import concourse.bacc as _bacc
    from concourse import mybir as _mybir
    from concourse.bass_utils import run_bass_kernel_spmd as _run

    nc = _bacc.Bacc("TRN2", target_bir_lowering=False, num_devices=1)
    arrays, args = {}, []
    for name in _INS:
        a = _np.ascontiguousarray(inputs[name])
        arrays[f"in_{name}_dram"] = a
        args.append(nc.dram_tensor(f"in_{name}_dram", a.shape, _mybir.dt.from_np(a.dtype), kind="ExternalInput").ap())
    for i, (shape, dtype) in enumerate(_OUTS):
        dt = _mybir.dt.from_np(_np.dtype(dtype))
        args.append(nc.dram_tensor(f"out_{i}_dram", shape, dt, kind="ExternalOutput").ap())
    bass_layer(nc, *args)
    r = _run(nc, [arrays], core_ids=[0])
    return r.results[0]["out_0_dram"]
```
